# Optimizing a Trainium2 kernel written in Bass

```python
import numpy as np
import jax
import jax.numpy as jnp

def _softmax(x, axis=-1):
    return jax.nn.softmax(x, axis=axis)

def _gelu(x):
    return jax.nn.gelu(x, approximate=True)

def _silu(x):
    return jax.nn.silu(x)

def _sigmoid(x):
    return jax.nn.sigmoid(x)

def _layernorm(x, axis=-1, eps=1e-05):
    m = jnp.mean(x, axis=axis, keepdims=True)
    v = jnp.var(x, axis=axis, keepdims=True)
    return (x - m) / jnp.sqrt(v + eps)

def _scatter_add(tgt, idx, src, axis=0):
    return tgt.at[idx].add(src)

def _segment_sum(src, seg, n):
    return jax.ops.segment_sum(src, seg, n)
kernel_name = 'mk_macaron_d1_jaxref_r4_1d75a3'

def setup_inputs(seed: int=0):
    np.random.seed(seed)
    _w = jnp.asarray

    def _L0_attn_setup():
        import jax, jax.numpy as jnp
        import numpy as np
        EMB = 1024
        HEADS = 32
        SCALE = 4
        D = EMB // HEADS
        HKV = HEADS // SCALE
        B, S = (2, 512)
        key = jax.random.key(seed)
        ks = jax.random.split(key, 7)
        std = 0.02
        return {'x': jax.random.normal(ks[0], (B, S, EMB), jnp.float32), 'Wq': jax.random.normal(ks[1], (EMB, D, HEADS), jnp.float32) * std, 'bq': jnp.zeros((D, HEADS), jnp.float32), 'Wk': jax.random.normal(ks[2], (EMB, D, HKV), jnp.float32) * std, 'bk': jnp.zeros((D, HKV), jnp.float32), 'Wv': jax.random.normal(ks[3], (EMB, D, HKV), jnp.float32) * std, 'bv': jnp.zeros((D, HKV), jnp.float32)}
    _L0_attn_in = _L0_attn_setup()

    def _L0_ffn_setup():
        import jax, jax.numpy as jnp
        import numpy as np
        IN_F = 1024
        OUT_F = 1024
        N_CLUSTERS = 64
        THRESHOLD = 0.01
        TEMPERATURE = 0.1
        BATCH, SEQ = (4, 512)
        key = jax.random.key(seed)
        k1, k2, k3, k4, k5 = jax.random.split(key, 5)
        s = 1.0 / np.sqrt(IN_F)
        return {'input': jax.random.normal(k1, (BATCH, SEQ, IN_F), dtype=jnp.float32), 'weight': jax.random.normal(k2, (OUT_F, IN_F), dtype=jnp.float32) * s, 'bias': jax.random.uniform(k3, (OUT_F,), dtype=jnp.float32, minval=-s, maxval=s), 'centroids': jax.random.normal(k4, (N_CLUSTERS, IN_F), dtype=jnp.float32) * s, 'assignments': jax.random.randint(k5, (OUT_F,), 0, N_CLUSTERS, dtype=jnp.int32)}
    _L0_ffn_in = _L0_ffn_setup()
    _d = {'L0_attn_x': _L0_attn_in['x'], 'L0_attn_Wq': _L0_attn_in['Wq'], 'L0_attn_bq': _L0_attn_in['bq'], 'L0_attn_Wk': _L0_attn_in['Wk'], 'L0_attn_bk': _L0_attn_in['bk'], 'L0_attn_Wv': _L0_attn_in['Wv'], 'L0_attn_bv': _L0_attn_in['bv'], 'L0_ffn_weight': _L0_ffn_in['weight'], 'L0_ffn_bias': _L0_ffn_in['bias'], 'L0_ffn_centroids': _L0_ffn_in['centroids'], 'L0_ffn_assignments': _L0_ffn_in['assignments']}
    _x0 = _d['L0_attn_x']
    _d['L0_attn_x'] = jax.random.normal(jax.random.fold_in(jax.random.key(seed), 1), (4, 1024, 1024), dtype=_x0.dtype)
    del _x0
    return _d

def reference(L0_attn_x, L0_attn_Wq, L0_attn_bq, L0_attn_Wk, L0_attn_bk, L0_attn_Wv, L0_attn_bv, L0_ffn_weight, L0_ffn_bias, L0_ffn_centroids, L0_ffn_assignments):

    def _L0_attn_ref(x, Wq, bq, Wk, bk, Wv, bv):
        import jax, jax.numpy as jnp
        import numpy as np
        EMB = 1024
        HEADS = 32
        SCALE = 4
        D = EMB // HEADS
        HKV = HEADS // SCALE
        B, S = (2, 512)
        q = jnp.einsum('bse,edh->bsdh', x, Wq) + bq
        k = jnp.einsum('bse,edh->bsdh', x, Wk) + bk
        v = jnp.einsum('bse,edh->bsdh', x, Wv) + bv
        k = jnp.repeat(k, SCALE, axis=-1)
        v = jnp.repeat(v, SCALE, axis=-1)
        scores = jnp.einsum('bsdh,bseh->bsde', q, k) / np.float32(np.sqrt(D))
        attn = jax.nn.softmax(scores, axis=-1)
        out = jnp.einsum('bsde,bseh->bsdh', attn, v)
        return out.reshape(x.shape[:-1] + (EMB,))

    def _L0_ffn_ref(input, weight, bias, centroids, assignments):
        import jax, jax.numpy as jnp
        import numpy as np
        IN_F = 1024
        OUT_F = 1024
        N_CLUSTERS = 64
        THRESHOLD = 0.01
        TEMPERATURE = 0.1
        BATCH, SEQ = (4, 512)
        shape = input.shape
        x = input.reshape(-1, shape[-1])
        dots = jax.nn.softmax(x @ centroids.T / TEMPERATURE, axis=-1)
        hits = dots > THRESHOLD
        query_sel = jnp.any(hits, axis=1)
        cluster_sel = jnp.any(hits, axis=0)
        row_sel = cluster_sel[assignments]
        dense = x @ weight.T + bias
        out = jnp.where(query_sel[:, None] & row_sel[None, :], dense, jnp.zeros((), dense.dtype))
        return out.reshape(*shape[:-1], -1)
    x = L0_attn_x
    x = x + 0.5 * _L0_ffn_ref(_layernorm(x, axis=-1), L0_ffn_weight, L0_ffn_bias, L0_ffn_centroids, L0_ffn_assignments)
    x = x + _L0_attn_ref(_layernorm(x, axis=-1), L0_attn_Wq, L0_attn_bq, L0_attn_Wk, L0_attn_bk, L0_attn_Wv, L0_attn_bv)
    x = x + 0.5 * _L0_ffn_ref(_layernorm(x, axis=-1), L0_ffn_weight, L0_ffn_bias, L0_ffn_centroids, L0_ffn_assignments)
    return x

_drawn_inputs = setup_inputs


def setup_inputs(seed=0):
    import zlib

    import numpy as np

    out = dict(_drawn_inputs(seed))
    spreads = {'L0_attn_bq': (0.0, 0.8), 'L0_attn_bk': (0.0, 0.8), 'L0_attn_bv': (0.0, 0.577)}
    factors = {'L0_ffn_bias': 4.42}
    for name, (base, spread) in spreads.items():
        noise = np.random.default_rng([zlib.crc32(name.encode()), seed]).standard_normal(out[name].shape)
        drawn = base * np.exp(spread * noise) if base else spread * noise
        out[name] = jnp.asarray(drawn.astype(out[name].dtype))
    for name, factor in factors.items():
        out[name] = (out[name] * factor).astype(out[name].dtype)
    return out
```

```python
import numpy as np
import concourse.bass as bass
from concourse import mybir
from contextlib import ExitStack

F32 = mybir.dt.float32
F32R = mybir.dt.float32r
I32 = mybir.dt.int32
ALU = mybir.AluOpType
ACT = mybir.ActivationFunctionType
AX = mybir.AxisListType
ds = bass.ds

P = 128
EMB = 1024
KB = EMB // P
HEADS = 32
SCALE = 4
D = EMB // HEADS
HKV = HEADS // SCALE
PROJ = 3 * HKV * D
NCL = 64
THRESHOLD = 0.01
INV_TEMPERATURE = 10.0
EPS = 1e-5
T4, R4, J8 = 4, 4, 8
SLOTS = 5
HALF = 512


def macaron_kernel(nc, x_in, Wq, bq, Wk, bk, Wv, bv, W, ffn_bias, centroids, assignments, out):
    x_d = x_in.rearrange("b (n p) e -> (b n) p e", p=P)
    out_d = out.rearrange("b (n p) e -> (b n) p e", p=P)
    NT = x_d.shape[0]

    x2_d = nc.dram_tensor("x2_scratch", (NT, P, EMB), F32, kind="Internal").ap()
    qkv_d = nc.dram_tensor("qkv_scratch", (NT, 3 * HKV, P, D), F32, kind="Internal").ap()
    o_d = nc.dram_tensor("o_scratch", (NT, HKV, P, D), F32, kind="Internal").ap()

    ctx = ExitStack()
    with ctx:
        def sb(name, shape, dt=F32):
            return ctx.enter_context(nc.sbuf_tensor(name, shape, dt))

        def sem(name):
            return ctx.enter_context(nc.semaphore(name))

        w_hi, w_lo = sb("w_hi", [P, KB, EMB], F32R), sb("w_lo", [P, KB, EMB], F32R)
        proj_hi, proj_lo = sb("proj_hi", [P, KB, PROJ], F32R), sb("proj_lo", [P, KB, PROJ], F32R)
        cen_hi, cen_lo = sb("cen_hi", [P, KB, NCL], F32R), sb("cen_lo", [P, KB, NCL], F32R)
        y_hi = [sb(f"y_hi{n}", [P, KB, P], F32R) for n in range(2)]
        y_lo = [sb(f"y_lo{n}", [P, KB, P], F32R) for n in range(2)]

        work = sb("work", [P, 14592])
        x_ring = work[:, 0:SLOTS * EMB].rearrange("p (s n) -> p s n", n=EMB)
        y_tok = [work[:, 5120:6144], work[:, 6144:7168]]
        probs = work[:, 7168:8192]
        probs_t = work[:, 8192:9216]
        v_diag = work[:, 9216:10240]
        q_diag = work[:, 10240:11264]
        qkv_tok = work[:, 11264:12032]
        k_head = work[:, 12032:12288]
        v_head = work[:, 12288:12544]
        mask_half = work[:, 12544:13568]
        bias_half = work[:, 13568:14592]
        w_raw = work[:, 0:8192].rearrange("p (o n) -> p o n", n=EMB)
        proj_raw = [work[:, 8192:9728], work[:, 9728:11264]]
        proj_sum = [qkv_tok, work[:, 12544:13312]]
        cen_raw = work[0:NCL, 13568:14592]
        assign_int = work[0:NCL, 7168:8192].bitcast(I32)
        onehot = work[0:NCL, 8192:9216]

        proj_bias = sb("proj_bias", [P, PROJ])
        q_head = sb("q_head", [P, HKV * D])
        own_t = sb("own_t", [P, T4])
        ffn_part = sb("ffn_part", [P, 2, HALF])
        o_head = sb("o_head", [P, HKV * D])
        o_tok = sb("o_tok", [P, HKV * D])
        ident = sb("ident", [P, P])
        ones = sb("ones", [P, P])
        minus_half = sb("minus_half", [P, 1])
        cluster_id = sb("cluster_id", [NCL, 1])
        cluster_int = sb("cluster_int", [NCL, 1], I32)
        cluster_on = sb("cluster_on", [NCL, P])
        hit = sb("hit", [P, NCL])
        best = [sb(f"best{n}", [P, NCL]) for n in range(2)]
        bn = [sb(f"bn{n}", [P, 2, 6]) for n in range(2)]
        moments = [sb(f"moments{n}", [P, 2]) for n in range(2)]
        var_eps = [sb(f"var_eps{n}", [P, 1]) for n in range(2)]
        rstd = [sb(f"rstd{n}", [P, 1]) for n in range(2)]
        stats = [sb(f"stats{n}", [P, NT, 2]) for n in range(2)]
        token_on = [sb(f"token_on{n}", [P, NT]) for n in range(2)]
        neg_max = sb("neg_max", [P, 1])
        exp_bias = sb("exp_bias", [P, 1])
        exp_c = sb("exp_c", [P, NCL])
        prob_c = sb("prob_c", [P, NCL])
        exp_sum = sb("exp_sum", [P, 1])
        exp_inv = sb("exp_inv", [P, 1])
        prob_max = sb("prob_max", [P, 1])
        row_max = sb("row_max", [P, HEADS])
        row_sum = sb("row_sum", [P, HEADS])
        row_inv = sb("row_inv", [P, HEADS])

        ps_t = ctx.enter_context(nc.psum_tensor("ps_t", [P, KB, P], F32))
        ps_a = ctx.enter_context(nc.psum_tensor("ps_a", [P, 2 * HALF], F32))
        ps_b = ctx.enter_context(nc.psum_tensor("ps_b", [P, 2 * HALF], F32))
        ps_s = ctx.enter_context(nc.psum_tensor("ps_s", [P, 2 * HALF], F32))

        def slot(t):
            return x_ring[:, ds(t % SLOTS, 1), :].rearrange("p a n -> p (a n)")

        def wait(eng, semaphore, value):
            if not isinstance(value, int) or value > 0:
                eng.wait_ge(semaphore, value)

        held = sem("held")

        def wait_alone(eng, semaphore, value):
            eng.wait_ge(semaphore, value)
            eng.sem_inc(held, 1)

        def product(pe, acc, hi, lo, w_h, w_l, cols):
            for k in range(KB):
                pe.matmul(acc, hi[:, k, :], w_h[:, k, cols], start=(k == 0), stop=False)
                pe.matmul(acc, hi[:, k, :], w_l[:, k, cols], start=False, stop=False)
                last = pe.matmul(acc, lo[:, k, :], w_h[:, k, cols], start=False, stop=(k == KB - 1))
            return last

        def transposes(pe, src):
            for k in range(KB):
                last = pe.transpose(ps_t[:, k, :], src[:, k * P:(k + 1) * P], ident[:, :])
            return last

        w_loaded = [sem(f"w_loaded{n}") for n in range(2)]
        cen_loaded = sem("cen_loaded")
        raw_loaded = [sem(f"raw_loaded{n}") for n in range(2)]
        bias_loaded = sem("bias_loaded")
        const_set = sem("const_set")
        ident_set = sem("ident_set")
        wt_done, wt_hi, wt_lo = sem("wt_done"), sem("wt_hi"), sem("wt_lo")
        q_summed, kv_moved = sem("q_summed"), sem("kv_moved")
        proj_hi_set, proj_lo_set = sem("proj_hi_set"), sem("proj_lo_set")
        bias_set = sem("bias_set")

        Wq_k = Wq.rearrange("(k p) d h -> k p (d h)", p=P)
        Wk_k = Wk.rearrange("(k p) d h -> k p (d h)", p=P)
        Wv_k = Wv.rearrange("(k p) d h -> k p (d h)", p=P)
        W_o = W.rearrange("(o p) i -> p o i", p=P)
        HD = HKV * D

        with nc.Block() as block:
            @block.sync
            def _(sp):
                sp.dma_start(cen_raw, centroids).then_inc(cen_loaded, 16)
                for n in range(2):
                    sp.dma_start(w_raw[:, 4 * n:4 * n + 4, :], W_o[:, 4 * n:4 * n + 4, :]).then_inc(w_loaded[n], 16)
                for k in range(KB + 1):
                    n = k % 2
                    if k >= 2:
                        sp.wait_ge(q_summed, k - 1)
                        sp.wait_ge(kv_moved, k - 1)
                        sp.wait_ge(raw_loaded[n], 48 * (k // 2))
                    if k < KB:
                        srcs = [Wq_k[k], Wk_k[k], Wv_k[k]]
                    else:
                        srcs = [b.rearrange("d h -> (d h)").partition_broadcast(P) for b in (bq, bk, bv)]
                    for src, a, b in zip(srcs, (0, EMB, EMB + HD), (EMB, EMB + HD, EMB + 2 * HD)):
                        sp.dma_start(proj_raw[n][:, a:b], src).then_inc(raw_loaded[n], 16)

            @block.gpsimd
            def _(pool):
                pool.memset(ident[:, :], 0.0).then_inc(ident_set, 1)
                pool.memset(ones[:, :], 1.0)
                pool.memset(minus_half[:, :], -0.5)
                pool.iota(cluster_int[:, :], pattern=[[0, 1]], base=0, channel_multiplier=1).then_inc(const_set, 1)
                pool.wait_ge(ident_set, 1)
                pool.affine_select(out=ident[:, :], in_=ident[:, :], compare_op=ALU.not_equal, fill=1.0, base=0,
                                   pattern=[[-1, P]], channel_multiplier=1).then_inc(ident_set, 1)
                for k in range(KB):
                    pool.wait_ge(proj_hi_set, k + 1)
                    pool.tensor_tensor(proj_lo[:, k, :], proj_sum[k % 2], proj_hi[:, k, :].bitcast(F32),
                                       ALU.subtract).then_inc(proj_lo_set, 1)

            @block.scalar
            def _(act):
                act.wait_ge(wt_done, 1)
                act.copy(cen_hi[:, :, :], ps_t[:, :, 0:NCL]).then_inc(wt_hi, 1)
                for o in range(KB):
                    act.wait_ge(wt_done, o + 2)
                    act.copy(w_hi[:, :, o * P:(o + 1) * P], ps_t[:, :, :]).then_inc(wt_hi, 1)
                for k in range(KB + 1):
                    raw, dst = proj_raw[k % 2], (proj_sum[k % 2] if k < KB else proj_bias)
                    act.wait_ge(raw_loaded[k % 2], 48 * (k // 2 + 1))
                    if 2 <= k < KB:
                        act.wait_ge(proj_lo_set, k - 1)
                    for a, b in ((EMB, HD), (EMB + HD, 2 * HD)):
                        moved = act.copy(dst[:, b:b + HD].rearrange("p (g d) -> p d g", g=HKV),
                                         raw[:, a:a + HD].rearrange("p (d g) -> p d g", g=HKV))
                    moved.then_inc(kv_moved, 1)
                    if k < KB:
                        act.wait_ge(q_summed, k + 1)
                        act.wait_ge(kv_moved, k + 1)
                        act.copy(proj_hi[:, k, :], proj_sum[k % 2]).then_inc(proj_hi_set, 1)

            @block.vector
            def _(dve):
                dve.memset(best[0][:, :], 0.0)
                dve.memset(best[1][:, :], 0.0)
                dve.wait_ge(ident_set, 2)
                dve.reduce_sum(own_t[:, :], ident[:, :].rearrange("p (c t) -> p t c", t=T4), AX.X)
                dve.wait_ge(const_set, 1)
                dve.tensor_copy(cluster_id[:, :], cluster_int[:, :])
                dve.wait_ge(wt_hi, 1)
                dve.tensor_tensor(cen_lo[:, :, :], ps_t[:, :, 0:NCL], cen_hi[:, :, :].bitcast(F32),
                                  ALU.subtract).then_inc(wt_lo, 1)
                for o in range(KB):
                    dve.wait_ge(wt_hi, o + 2)
                    w_block = w_hi[:, :, o * P:(o + 1) * P]
                    dve.tensor_tensor(w_lo[:, :, o * P:(o + 1) * P], ps_t[:, :, :], w_block.bitcast(F32),
                                      ALU.subtract).then_inc(wt_lo, 1)
                for k in range(KB + 1):
                    raw, dst = proj_raw[k % 2], (proj_sum[k % 2] if k < KB else proj_bias)
                    dve.wait_ge(raw_loaded[k % 2], 48 * (k // 2 + 1))
                    if 2 <= k < KB:
                        dve.wait_ge(proj_lo_set, k - 1)
                    dve.tensor_reduce(dst[:, 0:HD].rearrange("p (g d) -> p g d", g=HKV),
                                      raw[:, 0:EMB].rearrange("p (d g r) -> p g d r", g=HKV, r=SCALE),
                                      axis=AX.X, op=ALU.add).then_inc(q_summed, 1)

            @block.tensor
            def _(pe):
                pe.wait_ge(ident_set, 2)
                pe.wait_ge(cen_loaded, 16)
                for k in range(KB):
                    last = pe.transpose(ps_t[:, k, 0:NCL], cen_raw[:, k * P:(k + 1) * P], ident[0:NCL, 0:NCL])
                last.then_inc(wt_done, 1)
                for o in range(KB):
                    if o % 4 == 0:
                        pe.wait_ge(w_loaded[o // 4], 16)
                    pe.wait_ge(wt_lo, o + 1)
                    transposes(pe, w_raw[:, o, :]).then_inc(wt_done, 1)

        def layer_norm_stats(dve, x, n, step, t, var_ready):
            dve.bn_stats(bn[n][:, 0, :], x[:, 0:HALF])
            dve.bn_stats(bn[n][:, 1, :], x[:, HALF:EMB]).then_inc(step, 1)
            wait_alone(dve, step, 2 * t + 1)
            dve.bn_aggr(moments[n][:, :], bn[n][:, :, :]).then_inc(step, 1)
            dve.wait_ge(step, 2 * t + 2)
            dve.tensor_scalar_add(var_eps[n][:, :], moments[n][:, 1:2], EPS).then_inc(var_ready, 1)

        def cluster_max(dve, scores, step, t, ready):
            dve.tensor_reduce(neg_max[:, :], scores, axis=AX.X, op=ALU.max, negate=True).then_inc(step, 1)
            dve.wait_ge(step, 3 * t + 1)
            dve.tensor_scalar_mul(exp_bias[:, :], neg_max[:, :], INV_TEMPERATURE).then_inc(ready, 1)

        def cluster_probs(dve, n, step, t, done):
            dve.reciprocal(exp_inv[:, :], exp_sum[:, :]).then_inc(step, 1)
            dve.wait_ge(step, 3 * t + 2)
            dve.tensor_scalar(prob_c[:, :], exp_c[:, :], exp_inv[:, :], None, ALU.mult).then_inc(step, 1)
            dve.wait_ge(step, 3 * t + 3)
            dve.tensor_tensor(best[n][:, :], best[n][:, :], prob_c[:, :], ALU.max)
            dve.reduce_max(prob_max[:, :], prob_c[:, :], AX.X).then_inc(done, 1)

        def token_select(dve, n, t, done):
            dve.wait_ge(done, t + 1)
            dve.tensor_scalar(token_on[n][:, ds(t, 1)], prob_max[:, :], THRESHOLD, None, ALU.is_gt)

        s_x_loaded = [sem(f"s_x_loaded{n}") for n in range(2)]
        s_step, s_var, s_rstd, s_stat = sem("s_step"), sem("s_var"), sem("s_rstd"), sem("s_stat")
        s_y, s_t, s_hi, s_lo = sem("s_y"), sem("s_t"), sem("s_hi"), sem("s_lo")
        s_c, s_cstep, s_cmax, s_cexp, s_cdone = (sem("s_c"), sem("s_cstep"), sem("s_cmax"), sem("s_cexp"),
                                                sem("s_cdone"))

        def scan(eng, emit):
            for i in (-1, 0, 1, 2):
                emit(i, i % 2, lambda t: 0 <= t < NT)
            with eng.Fori(1, (NT - 2) // 2) as m:
                for u in range(2):
                    emit(m * 2 + (1 + u), (1 + u) % 2, lambda t: True)
            for i in (NT - 1, NT):
                emit(i, i % 2, lambda t: 0 <= t < NT)

        with nc.Block() as block:
            @block.sync
            def _(sp):
                def load(t, n):
                    if not isinstance(t, int) or t >= 2:
                        wait_alone(sp, s_x_loaded[n], (t - n) * 8)
                    if not isinstance(t, int) or t >= 4:
                        sp.wait_ge(s_y, t - 3)
                    sp.dma_start(x_ring[:, ds(t % 4, 1), :].rearrange("p a n -> p (a n)"),
                                 x_d[ds(t, 1)].rearrange("a p n -> (a p) n")).then_inc(s_x_loaded[n], 16)
                for t in range(4):
                    load(t, t % 2)
                with sp.Fori(2, NT // 2) as m:
                    for n in range(2):
                        load(m * 2 + n, n)

            @block.gpsimd
            def _(pool):
                pool.memset(v_diag, 0.0)

                def power(t):
                    pool.wait_ge(s_var, t + 1)
                    pool.tensor_tensor(rstd[0][:, :], var_eps[0][:, :], minus_half[:, :], ALU.pow).then_inc(s_rstd, 1)
                with pool.Fori(0, NT) as t:
                    power(t)

            @block.vector
            def _(dve):
                def step(i, par, ok):
                    if ok(i + 1):
                        t, n = i + 1, (par + 1) % 2
                        x = x_ring[:, ds(t % 4, 1), :].rearrange("p a n -> p (a n)")
                        dve.wait_ge(s_x_loaded[n], (t - n) * 8 + 16)
                        layer_norm_stats(dve, x, 0, s_step, t, s_var)
                    if ok(i):
                        dve.wait_ge(s_hi, i + 1)
                        dve.tensor_tensor(y_lo[par][:, :, :], ps_t[:, :, :], y_hi[par][:, :, :].bitcast(F32),
                                          ALU.subtract).then_inc(s_lo, 1)
                    if ok(i + 1):
                        dve.wait_ge(s_rstd, t + 1)
                        wait(dve, s_t, t - 1)
                        dve.tensor_scalar(y_tok[n], x, moments[0][:, 0:1], rstd[0][:, :], ALU.subtract,
                                          ALU.mult).then_inc(s_y, 1)
                        dve.tensor_copy(stats[0][:, ds(t, 1), 0:1].rearrange("p a b -> p (a b)"), moments[0][:, 0:1])
                        dve.tensor_copy(stats[0][:, ds(t, 1), 1:2].rearrange("p a b -> p (a b)"), rstd[0][:, :])
                    if ok(i - 1):
                        t, n = i - 1, (par + 1) % 2
                        dve.wait_ge(s_c, t + 1)
                        cluster_max(dve, (ps_a, ps_b)[n][:, 0:NCL], s_cstep, t, s_cmax)
                        dve.wait_ge(s_cexp, t + 1)
                        cluster_probs(dve, 0, s_cstep, t, s_cdone)
                        token_select(dve, 0, t, s_cdone)
                scan(dve, step)

            @block.scalar
            def _(act):
                def step(i, par, ok):
                    if ok(i):
                        act.wait_ge(s_t, i + 1)
                        wait(act, s_c, i - 1)
                        act.copy(y_hi[par][:, :, :], ps_t[:, :, :]).then_inc(s_hi, 1)
                    if ok(i - 1):
                        t, n = i - 1, (par + 1) % 2
                        act.wait_ge(s_cmax, t + 1)
                        act.activation(exp_c[:, :], (ps_a, ps_b)[n][:, 0:NCL], ACT.Exp, bias=exp_bias[:, :],
                                       scale=INV_TEMPERATURE, accum_out=exp_sum[:, :]).then_inc(s_cexp, 1)
                scan(act, step)

            @block.tensor
            def _(pe):
                def step(i, par, ok):
                    if ok(i):
                        pe.wait_ge(s_y, i + 1)
                        wait(pe, s_lo, i)
                        transposes(pe, y_tok[par]).then_inc(s_t, 1)
                    if ok(i - 1):
                        t, n = i - 1, (par + 1) % 2
                        pe.wait_ge(s_lo, t + 1)
                        wait(pe, s_cexp, t - 1)
                        product(pe, (ps_a, ps_b)[n][:, 0:NCL], y_hi[n], y_lo[n], cen_hi, cen_lo,
                                slice(0, NCL)).then_inc(s_c, 1)
                scan(pe, step)

        def select(n):
            m_bias, m_assign = sem(f"m_bias{n}"), sem(f"m_assign{n}")
            m_hit, m_count, m_on, m_step = (sem(f"m_hit{n}"), sem(f"m_count{n}"), sem(f"m_on{n}"),
                                            sem(f"m_step{n}"))
            m_rows, m_mask = sem(f"m_rows{n}"), sem(f"m_mask{n}")
            with nc.Block() as block:
                @block.sync
                def _(sp):
                    sp.dma_start(assign_int, assignments.partition_broadcast(NCL)).then_inc(m_assign, 16)
                    sp.dma_start(bias_half, ffn_bias.partition_broadcast(P)).then_inc(m_bias, 16)

                @block.vector
                def _(dve):
                    dve.tensor_scalar(hit[:, :], best[n][:, :], THRESHOLD, None, ALU.is_gt).then_inc(m_hit, 1)
                    dve.wait_ge(m_assign, 16)
                    dve.tensor_copy(onehot, assign_int).then_inc(m_step, 1)
                    dve.wait_ge(m_step, 1)
                    dve.tensor_scalar(onehot, onehot, cluster_id[:, :], None, ALU.is_equal).then_inc(m_step, 1)
                    dve.wait_ge(m_count, 1)
                    dve.tensor_scalar(cluster_on[:, :], ps_b[0:NCL, 0:P], 1.0, 0.5, ALU.min, ALU.mult).then_inc(m_on, 1)
                    dve.wait_ge(m_rows, 1)
                    dve.tensor_copy(mask_half, ps_a[:, :]).then_inc(m_mask, 1)
                    dve.wait_ge(m_mask, 1)
                    dve.wait_ge(m_bias, 16)
                    dve.tensor_tensor(bias_half, bias_half, mask_half, ALU.mult)

                @block.tensor
                def _(pe):
                    pe.wait_ge(m_hit, 1)
                    pe.matmul(ps_b[0:NCL, 0:P], hit[:, :], ones[:, :], start=True, stop=True).then_inc(m_count, 1)
                    pe.wait_ge(m_on, 1)
                    pe.wait_ge(m_step, 2)
                    for h in range(2):
                        last = pe.matmul(ps_a[:, h * HALF:(h + 1) * HALF], cluster_on[:, :],
                                         onehot[:, h * HALF:(h + 1) * HALF], start=True, stop=True)
                    last.then_inc(m_rows, 1)

        select(0)

        x_loaded, x2_ready, x2_stored = sem("x_loaded"), sem("x2_ready"), sem("x2_stored")
        y1_ready, y2_ready, y3_ready = sem("y1_ready"), sem("y2_ready"), sem("y3_ready")
        t1_done, t2_done, t3_done = sem("t1_done"), sem("t2_done"), sem("t3_done")
        hi1, hi2, hi3 = sem("hi1"), sem("hi2"), sem("hi3")
        lo1, lo2, lo3 = sem("lo1"), sem("lo2"), sem("lo3")
        ffn_done, ffn_read, x1_step = sem("ffn_done"), sem("ffn_read"), sem("x1_step")
        ln2_step, var2, rstd2 = sem("ln2_step"), sem("var2"), sem("rstd2")
        ln3_step, var3, rstd3 = sem("ln3_step"), sem("var3"), sem("rstd3")
        proj_done, proj_read, qkv_stored = sem("proj_done"), sem("proj_read"), sem("qkv_stored")
        q_loaded, k_loaded, v_loaded = sem("q_loaded"), sem("k_loaded"), sem("v_loaded")
        q_diag_ready, v_diag_ready = sem("q_diag_ready"), sem("v_diag_ready")
        scores_done, scores_read, exp_ready = sem("scores_done"), sem("scores_read"), sem("exp_ready")
        soft_step, probs_ready, heads_done = sem("soft_step"), sem("probs_ready"), sem("heads_done")
        o_ready, o_stored, o_loaded = sem("o_ready"), sem("o_stored"), sem("o_loaded")
        c_done, c_step, c_max, c_exp, c_probs = sem("c_done"), sem("c_step"), sem("c_max"), sem("c_exp"), sem("c_probs")

        def main(eng, emit):
            for i in range(-1, 4):
                emit(i, lambda t: 0 <= t < NT)
            with eng.Fori(4, NT - 2) as i:
                emit(i, lambda t: True)
            for i in range(NT - 2, NT + 3):
                emit(i, lambda t: 0 <= t < NT)

        def prob_block(r, j):
            return (r % 2) * HALF + (r // 2) * J8 * D + j * D

        with nc.Block() as block:
            @block.sync
            def _(sp):
                def load(t):
                    wait(sp, x_loaded, 16 * t)
                    sp.dma_start(slot(t), x_d[ds(t, 1)].rearrange("a p n -> (a p) n")).then_inc(x_loaded, 16)

                def step(i, ok):
                    if ok(i - 3):
                        t = i - 3
                        sp.wait_ge(o_ready, t + 1)
                        sp.dma_start(o_d[ds(t, 1)].rearrange("a g (t r j) d -> r (a g t) (j d)", t=T4, r=R4),
                                     o_head[:, :]).then_inc(o_stored, 16)
                        sp.wait_ge(o_stored, 16 * t + 16)
                        wait(sp, x2_ready, t)
                        sp.dma_start(o_tok[:, :].rearrange("p (g d) -> p g d", g=HKV),
                                     o_d[ds(t, 1)].rearrange("a g k d -> (a k) g d")).then_inc(o_loaded, 16)
                        sp.wait_ge(x2_ready, t + 1)
                        sp.dma_start(x2_d[ds(t, 1)].rearrange("a p n -> (a p) n"), slot(t)).then_inc(x2_stored, 16)
                    if ok(i + 2):
                        if ok(i - 3):
                            sp.wait_ge(x2_stored, 16 * (i - 2))
                            sp.wait_ge(y3_ready, i - 2)
                        load(i + 2)
                    if ok(i - 1):
                        t = i - 1
                        sp.wait_ge(proj_read, 2 * t + 2)
                        sp.dma_start(qkv_d[ds(t, 1)].rearrange("a s k e -> (a k) s e"),
                                     qkv_tok.rearrange("p (s e) -> p s e", e=D)).then_inc(qkv_stored, 16)
                        sp.wait_ge(qkv_stored, 16 * t + 16)
                        q, k, v = (qkv_d[ds(t, 1), HKV * s:HKV * (s + 1)] for s in range(3))
                        by_row_block = "a g (t r j) e -> r (a g t) (j e)"
                        wait(sp, q_diag_ready, t)
                        sp.dma_start(q_head[:, :], q.rearrange(by_row_block, t=T4, r=R4)).then_inc(q_loaded, 16)
                        wait(sp, scores_done, R4 * t)
                        sp.dma_start(k_head, k.rearrange(by_row_block, t=T4, r=R4)).then_inc(k_loaded, 16)
                        wait(sp, v_diag_ready, t)
                        sp.dma_start(v_head, v.rearrange("a g (n j) e -> (a n) g (j e)", j=J8)).then_inc(v_loaded, 16)
                load(0)
                main(sp, step)
                sp.wait_ge(x2_stored, 16 * NT)

            @block.gpsimd
            def _(pool):
                def step(i, ok):
                    if ok(i - 3):
                        pool.wait_ge(var3, i - 2)
                        pool.tensor_tensor(rstd[1][:, :], var_eps[1][:, :], minus_half[:, :], ALU.pow).then_inc(rstd3, 1)
                    if ok(i):
                        pool.wait_ge(var2, i + 1)
                        pool.tensor_tensor(rstd[0][:, :], var_eps[0][:, :], minus_half[:, :], ALU.pow).then_inc(rstd2, 1)
                main(pool, step)

            @block.scalar
            def _(act):
                def step(i, ok):
                    if ok(i - 2):
                        t = i - 2
                        act.wait_ge(q_loaded, 16 * t + 16)
                        wait(act, scores_done, R4 * t)
                        for b in range(T4):
                            last = act.activation(q_diag.rearrange("p (j t d) -> p j t d", t=T4, d=D)[:, :, b, :],
                                                  q_head[:, :].rearrange("p (j d) -> p j d", d=D), ACT.Identity,
                                                  scale=own_t[:, b:b + 1])
                        last.then_inc(q_diag_ready, 1)
                    if ok(i + 1):
                        act.wait_ge(t1_done, i + 2)
                        act.copy(y_hi[0][:, :, :], ps_t[:, :, :]).then_inc(hi1, 1)
                    if ok(i - 2):
                        act.wait_ge(scores_read, i - 1)
                        act.activation(probs, probs, ACT.Exp, scale=1.0 / float(np.sqrt(D))).then_inc(exp_ready, 1)
                    if ok(i - 3):
                        act.wait_ge(t3_done, i - 2)
                        act.copy(y_hi[1][:, :, :], ps_t[:, :, :]).then_inc(hi3, 1)
                    if ok(i - 2):
                        act.wait_ge(heads_done, i - 1)
                        wait(act, o_stored, 16 * (i - 2))
                        act.copy(o_head[:, :], ps_s[:, 0:HKV * D]).then_inc(o_ready, 1)
                    if ok(i - 3):
                        act.wait_ge(c_max, i - 2)
                        wait(act, c_probs, i - 3)
                        act.activation(exp_c[:, :], ps_a[:, 0:NCL], ACT.Exp, bias=exp_bias[:, :],
                                       scale=INV_TEMPERATURE, accum_out=exp_sum[:, :]).then_inc(c_exp, 1)
                    if ok(i):
                        act.wait_ge(t2_done, i + 1)
                        act.copy(y_hi[1][:, :, :], ps_t[:, :, :]).then_inc(hi2, 1)
                main(act, step)

            @block.vector
            def _(dve):
                def low_part(n, hi_sem, lo_sem, t):
                    dve.wait_ge(hi_sem, t + 1)
                    dve.tensor_tensor(y_lo[n][:, :, :], ps_t[:, :, :], y_hi[n][:, :, :].bitcast(F32),
                                      ALU.subtract).then_inc(lo_sem, 1)

                def step(i, ok):
                    if ok(i + 1):
                        t = i + 1
                        dve.wait_ge(x_loaded, 16 * t + 16)
                        wait(dve, t2_done, i)
                        dve.tensor_scalar(y_tok[0], slot(t), stats[0][:, ds(t, 1), 0:1].rearrange("p a b -> p (a b)"),
                                          stats[0][:, ds(t, 1), 1:2].rearrange("p a b -> p (a b)"),
                                          ALU.subtract, ALU.mult).then_inc(y1_ready, 1)
                    if ok(i - 2):
                        t = i - 2
                        dve.wait_ge(v_loaded, 16 * t + 16)
                        wait(dve, heads_done, t)
                        for b in range(T4):
                            last = dve.transpose(v_diag[32 * b:32 * b + 32, b:EMB:T4], v_head[32 * b:32 * b + 32, :])
                        last.then_inc(v_diag_ready, 1)
                    if ok(i):
                        on = token_on[0][:, ds(i, 1)]
                        dve.scalar_tensor_tensor(slot(i), bias_half, on, slot(i), ALU.mult, ALU.add).then_inc(x1_step, 1)
                        dve.wait_ge(x1_step, 3 * i + 1)
                    if ok(i - 3):
                        t = i - 3
                        dve.wait_ge(o_loaded, 16 * t + 16)
                        x2 = slot(t)
                        x2_v = x2.rearrange("p (d g r) -> p d g r", g=HKV, r=SCALE)
                        o_v = o_tok[:, :].rearrange("p (g d) -> p d g", g=HKV).unsqueeze(3).to_broadcast([P, D, HKV, SCALE])
                        dve.tensor_tensor(x2_v, x2_v, o_v, ALU.add).then_inc(x2_ready, 1)
                        wait_alone(dve, x2_ready, t + 1)
                        layer_norm_stats(dve, x2, 1, ln3_step, t, var3)
                    if ok(i):
                        for n, h in enumerate((1, 0)):
                            cols = slice(h * HALF, (h + 1) * HALF)
                            dve.wait_ge(ffn_done, 2 * i + n + 1)
                            dve.scalar_tensor_tensor(ffn_part[:, n, :], ps_a[:, cols], on, mask_half[:, cols],
                                                     ALU.mult, ALU.mult).then_inc(ffn_read, 1)
                            dve.wait_ge(ffn_read, 2 * i + n + 1)
                            dve.tensor_tensor(slot(i)[:, cols], slot(i)[:, cols], ffn_part[:, n, :],
                                              ALU.add).then_inc(x1_step, 1)
                            if n == 0 and ok(i - 3):
                                t = i - 3
                                dve.wait_ge(rstd3, t + 1)
                                wait(dve, t3_done, t)
                                dve.tensor_scalar(y_tok[1], slot(t), moments[1][:, 0:1], rstd[1][:, :], ALU.subtract,
                                                  ALU.mult).then_inc(y3_ready, 1)
                                dve.tensor_copy(stats[1][:, ds(t, 1), 0:1].rearrange("p a b -> p (a b)"),
                                                moments[1][:, 0:1])
                                dve.tensor_copy(stats[1][:, ds(t, 1), 1:2].rearrange("p a b -> p (a b)"), rstd[1][:, :])
                        wait_alone(dve, x1_step, 3 * i + 3)
                        layer_norm_stats(dve, slot(i), 0, ln2_step, i, var2)
                    elif ok(i - 3):
                        t = i - 3
                        dve.wait_ge(rstd3, t + 1)
                        wait(dve, t3_done, t)
                        dve.tensor_scalar(y_tok[1], slot(t), moments[1][:, 0:1], rstd[1][:, :], ALU.subtract,
                                          ALU.mult).then_inc(y3_ready, 1)
                        dve.tensor_copy(stats[1][:, ds(t, 1), 0:1].rearrange("p a b -> p (a b)"), moments[1][:, 0:1])
                        dve.tensor_copy(stats[1][:, ds(t, 1), 1:2].rearrange("p a b -> p (a b)"), rstd[1][:, :])
                    if ok(i - 2):
                        t = i - 2
                        groups = "p (c e) -> p c e"
                        wide = [P, HEADS, D]
                        probs_v = probs.rearrange(groups, e=D)
                        scores_v = ps_s[:, :].rearrange(groups, e=D)
                        dve.wait_ge(scores_done, R4 * t + R4)
                        dve.reduce_max(row_max[:, :], scores_v, AX.X).then_inc(soft_step, 1)
                        dve.wait_ge(soft_step, 4 * t + 1)
                        dve.tensor_tensor(probs_v, scores_v, row_max[:, :].unsqueeze(2).to_broadcast(wide),
                                          ALU.subtract).then_inc(scores_read, 1)
                    if ok(i + 1):
                        low_part(0, hi1, lo1, i + 1)
                    if ok(i):
                        dve.wait_ge(rstd2, i + 1)
                        if ok(i + 1):
                            dve.wait_ge(t1_done, i + 2)
                        else:
                            dve.wait_ge(t1_done, NT)
                        dve.tensor_scalar(y_tok[0], slot(i), moments[0][:, 0:1], rstd[0][:, :], ALU.subtract,
                                          ALU.mult).then_inc(y2_ready, 1)
                    if ok(i - 2):
                        dve.wait_ge(exp_ready, t + 1)
                        dve.reduce_sum(row_sum[:, :], probs_v, AX.X).then_inc(soft_step, 1)
                        dve.wait_ge(soft_step, 4 * t + 2)
                        dve.reciprocal(row_inv[:, :], row_sum[:, :]).then_inc(soft_step, 1)
                        dve.wait_ge(soft_step, 4 * t + 3)
                        dve.tensor_tensor(probs_v, probs_v, row_inv[:, :].unsqueeze(2).to_broadcast(wide),
                                          ALU.mult).then_inc(soft_step, 1)
                        dve.wait_ge(soft_step, 4 * t + 4)
                        wait(dve, heads_done, t)
                        dve.transpose(probs_t, probs).then_inc(probs_ready, 1)
                    if ok(i - 1):
                        t = i - 1
                        wait(dve, qkv_stored, 16 * t)
                        for n, cols in enumerate((slice(0, HALF), slice(HALF, PROJ))):
                            dve.wait_ge(proj_done, 2 * t + n + 1)
                            dve.tensor_tensor(qkv_tok[:, cols], ps_b[:, cols], proj_bias[:, cols],
                                              ALU.add).then_inc(proj_read, 1)
                    if ok(i - 3):
                        t = i - 3
                        low_part(1, hi3, lo3, t)
                        dve.wait_ge(c_done, t + 1)
                        cluster_max(dve, ps_a[:, 0:NCL], c_step, t, c_max)
                    if ok(i):
                        low_part(1, hi2, lo2, i)
                    if ok(i - 3):
                        t = i - 3
                        dve.wait_ge(c_exp, t + 1)
                        cluster_probs(dve, 1, c_step, t, c_probs)
                        token_select(dve, 1, t, c_probs)
                main(dve, step)

            @block.tensor
            def _(pe):
                def step(i, ok):
                    if ok(i):
                        pe.wait_ge(lo1, i + 1)
                        wait(pe, ffn_read, 2 * i)
                        product(pe, ps_a[:, HALF:EMB], y_hi[0], y_lo[0], w_hi, w_lo,
                                slice(HALF, EMB)).then_inc(ffn_done, 1)
                        if ok(i - 4):
                            wait(pe, c_exp, i - 3)
                        product(pe, ps_a[:, 0:HALF], y_hi[0], y_lo[0], w_hi, w_lo,
                                slice(0, HALF)).then_inc(ffn_done, 1)
                    if ok(i - 2):
                        t = i - 2
                        pe.wait_ge(q_diag_ready, t + 1)
                        pe.wait_ge(k_loaded, 16 * t + 16)
                        wait(pe, o_ready, t)
                        for r in range(R4):
                            if r >= 2:
                                pe.wait_ge(scores_done, R4 * t + r - 1)
                            rows = slice(32 * r, 32 * r + 32)
                            for j in range(J8):
                                c = prob_block(r, j)
                                last = pe.matmul(ps_s[:, c:c + D], q_diag[rows, j * P:(j + 1) * P],
                                                 k_head[rows, j * D:(j + 1) * D], start=True, stop=True)
                            last.then_inc(scores_done, 1)
                    if ok(i + 1):
                        pe.wait_ge(y1_ready, i + 2)
                        wait(pe, lo2, i)
                        transposes(pe, y_tok[0]).then_inc(t1_done, 1)
                    if ok(i - 1):
                        t = i - 1
                        pe.wait_ge(lo2, t + 1)
                        wait(pe, proj_read, 2 * t)
                        for cols in (slice(0, HALF), slice(HALF, PROJ)):
                            product(pe, ps_b[:, cols], y_hi[1], y_lo[1], proj_hi, proj_lo,
                                    cols).then_inc(proj_done, 1)
                    if ok(i - 3):
                        pe.wait_ge(y3_ready, i - 2)
                        if ok(i + 1):
                            pe.wait_ge(lo1, i + 2)
                        else:
                            pe.wait_ge(lo2, min(i, NT))
                        transposes(pe, y_tok[1]).then_inc(t3_done, 1)
                    if ok(i - 2):
                        t = i - 2
                        pe.wait_ge(probs_ready, t + 1)
                        pe.wait_ge(v_diag_ready, t + 1)
                        for j in range(J8):
                            for r in range(R4):
                                c = prob_block(r, j)
                                last = pe.matmul(ps_s[32 * r:32 * r + 32, j * D:(j + 1) * D],
                                                 v_diag[:, (j * R4 + r) * 32:(j * R4 + r + 1) * 32],
                                                 probs_t[:, c:c + D], start=True, stop=True)
                        last.then_inc(heads_done, 1)
                    if ok(i - 3):
                        pe.wait_ge(lo3, i - 2)
                        pe.wait_ge(ffn_read, 2 * i + 2 if ok(i) else 2 * NT)
                        product(pe, ps_a[:, 0:NCL], y_hi[1], y_lo[1], cen_hi, cen_lo,
                                slice(0, NCL)).then_inc(c_done, 1)
                    if ok(i):
                        pe.wait_ge(y2_ready, i + 1)
                        if ok(i - 3):
                            pe.wait_ge(lo3, i - 2)
                        else:
                            pe.wait_ge(lo1, i + 2)
                        transposes(pe, y_tok[0]).then_inc(t2_done, 1)
                main(pe, step)

        select(1)

        f_x_loaded = [sem(f"f_x_loaded{n}") for n in range(2)]
        f_y, f_t, f_hi, f_lo = sem("f_y"), sem("f_t"), sem("f_hi"), sem("f_lo")
        f_ffn, f_read, f_step, f_out = sem("f_ffn"), sem("f_read"), sem("f_step"), sem("f_out")

        def finish(eng, emit):
            for i in (-2, -1, 0, 1):
                emit(i, i % 2, lambda t: 0 <= t < NT)
            with eng.Fori(1, (NT - 2) // 2) as m:
                for u in range(2):
                    emit(m * 2 + u, u, lambda t: True)
            for i in (NT - 2, NT - 1):
                emit(i, i % 2, lambda t: 0 <= t < NT)

        with nc.Block() as block:
            @block.sync
            def _(sp):
                def load(t, n):
                    wait(sp, f_x_loaded[n], (t - n) * 8)
                    sp.dma_start(slot(t), x2_d[ds(t, 1)].rearrange("a p n -> (a p) n")).then_inc(f_x_loaded[n], 16)

                def step(i, par, ok):
                    if ok(i):
                        wait_alone(sp, f_step, 3 * i + 3)
                        wait(sp, f_out, 16 * i)
                        sp.dma_start(out_d[ds(i, 1)].rearrange("a p n -> (a p) n"), slot(i)).then_inc(f_out, 16)
                    if ok(i + 4):
                        if ok(i - 1):
                            sp.wait_ge(f_out, 16 * i)
                        load(i + 4, par)
                load(0, 0)
                load(1, 1)
                for i in (-2, -1):
                    step(i, i % 2, lambda t: 0 <= t < NT)
                step(0, 0, lambda t: 0 <= t < NT)
                step(1, 1, lambda t: 0 <= t < NT)
                with sp.Fori(1, (NT - 4) // 2) as m:
                    for u in range(2):
                        step(m * 2 + u, u, lambda t: True)
                for i in range(NT - 4, NT):
                    step(i, i % 2, lambda t: 0 <= t < NT)
                sp.wait_ge(f_out, 16 * NT)

            @block.vector
            def _(dve):
                def step(i, par, ok):
                    if ok(i + 1):
                        n = (par + 1) % 2
                        dve.wait_ge(f_hi, i + 2)
                        dve.tensor_tensor(y_lo[n][:, :, :], ps_t[:, :, :], y_hi[n][:, :, :].bitcast(F32),
                                          ALU.subtract).then_inc(f_lo, 1)
                    if ok(i + 2):
                        t = i + 2
                        dve.wait_ge(f_x_loaded[par], (t - par) * 8 + 16)
                        wait(dve, f_t, i + 1)
                        dve.tensor_scalar(y_tok[par], slot(t), stats[1][:, ds(t, 1), 0:1].rearrange("p a b -> p (a b)"),
                                          stats[1][:, ds(t, 1), 1:2].rearrange("p a b -> p (a b)"),
                                          ALU.subtract, ALU.mult).then_inc(f_y, 1)
                    if ok(i):
                        acc = (ps_a, ps_b)[par]
                        on = token_on[1][:, ds(i, 1)]
                        dve.scalar_tensor_tensor(slot(i), bias_half, on, slot(i), ALU.mult, ALU.add).then_inc(f_step, 1)
                        dve.wait_ge(f_step, 3 * i + 1)
                        for h in range(2):
                            cols = slice(h * HALF, (h + 1) * HALF)
                            dve.wait_ge(f_ffn, 2 * i + h + 1)
                            dve.scalar_tensor_tensor(ffn_part[:, h, :], acc[:, cols], on, mask_half[:, cols],
                                                     ALU.mult, ALU.mult).then_inc(f_read, 1)
                            dve.wait_ge(f_read, 2 * i + h + 1)
                            dve.tensor_tensor(slot(i)[:, cols], slot(i)[:, cols], ffn_part[:, h, :],
                                              ALU.add).then_inc(f_step, 1)
                finish(dve, step)

            @block.scalar
            def _(act):
                def step(i, par, ok):
                    if ok(i + 1):
                        n = (par + 1) % 2
                        act.wait_ge(f_t, i + 2)
                        act.copy(y_hi[n][:, :, :], ps_t[:, :, :]).then_inc(f_hi, 1)
                finish(act, step)

            @block.tensor
            def _(pe):
                def step(i, par, ok):
                    if ok(i + 1):
                        n = (par + 1) % 2
                        pe.wait_ge(f_y, i + 2)
                        wait(pe, f_lo, i + 1)
                        transposes(pe, y_tok[n]).then_inc(f_t, 1)
                    if ok(i):
                        pe.wait_ge(f_lo, i + 1)
                        wait(pe, f_read, 2 * (i - 1))
                        for h in range(2):
                            cols = slice(h * HALF, (h + 1) * HALF)
                            product(pe, (ps_a, ps_b)[par][:, cols], y_hi[par], y_lo[par], w_hi, w_lo,
                                    cols).then_inc(f_ffn, 1)
                finish(pe, step)


_INS = ["L0_attn_x", "L0_attn_Wq", "L0_attn_bq", "L0_attn_Wk", "L0_attn_bk", "L0_attn_Wv", "L0_attn_bv",
        "L0_ffn_weight", "L0_ffn_bias", "L0_ffn_centroids", "L0_ffn_assignments"]


def kernel(**inputs):
    import numpy as _np
    import concourse.bacc as _bacc
    from concourse import mybir as _mybir
    from concourse.bass_utils import run_bass_kernel_spmd as _run

    nc = _bacc.Bacc("TRN2", target_bir_lowering=False, num_devices=1)
    arrays, args = {}, []
    for name in _INS:
        a = _np.ascontiguousarray(inputs[name])
        arrays[f"in_{name}"] = a
        args.append(nc.dram_tensor(f"in_{name}", a.shape, _mybir.dt.from_np(a.dtype), kind="ExternalInput").ap())
    shape = arrays["in_L0_attn_x"].shape
    args.append(nc.dram_tensor("out", shape, _mybir.dt.float32, kind="ExternalOutput").ap())
    macaron_kernel(nc, *args)
    r = _run(nc, [arrays], core_ids=[0])
    return r.results[0]["out"]
```

```python
import numpy as np
import concourse.bass as bass
from concourse import mybir
from contextlib import ExitStack

F32 = mybir.dt.float32
F32R = mybir.dt.float32r
I32 = mybir.dt.int32
ALU = mybir.AluOpType
ACT = mybir.ActivationFunctionType
AX = mybir.AxisListType
ds = bass.ds

P = 128
EMB = 1024
KB = EMB // P
HEADS = 32
SCALE = 4
D = EMB // HEADS
HKV = HEADS // SCALE
PROJ = 3 * HKV * D
NCL = 64
THRESHOLD = 0.01
INV_TEMPERATURE = 10.0
EPS = 1e-5
T4, R4, J8 = 4, 4, 8
SLOTS = 5
HALF = 512


def macaron_kernel(nc, x_in, Wq, bq, Wk, bk, Wv, bv, W, ffn_bias, centroids, assignments, out):
    x_d = x_in.rearrange("b (n p) e -> (b n) p e", p=P)
    out_d = out.rearrange("b (n p) e -> (b n) p e", p=P)
    NT = x_d.shape[0]

    x2_d = nc.dram_tensor("x2_scratch", (NT, P, EMB), F32, kind="Internal").ap()
    qkv_d = nc.dram_tensor("qkv_scratch", (NT, 3 * HKV, P, D), F32, kind="Internal").ap()
    o_d = nc.dram_tensor("o_scratch", (NT, HKV, P, D), F32, kind="Internal").ap()

    ctx = ExitStack()
    with ctx:
        def sb(name, shape, dt=F32):
            return ctx.enter_context(nc.sbuf_tensor(name, shape, dt))

        def sem(name):
            return ctx.enter_context(nc.semaphore(name))

        w_hi, w_lo = sb("w_hi", [P, KB, EMB], F32R), sb("w_lo", [P, KB, EMB], F32R)
        proj_hi, proj_lo = sb("proj_hi", [P, KB, PROJ], F32R), sb("proj_lo", [P, KB, PROJ], F32R)
        cen = sb("cen", [P, KB, 2 * NCL], F32R)
        y_hi = [sb(f"y_hi{n}", [P, KB, P], F32R) for n in range(2)]
        y_lo = [sb(f"y_lo{n}", [P, KB, P], F32R) for n in range(2)]

        work = sb("work", [P, 15360])
        x_ring = work[:, 0:SLOTS * EMB].rearrange("p (s n) -> p s n", n=EMB)
        y_tok = [work[:, 5120:6144], work[:, 6144:7168]]
        probs = work[:, 7168:8192]
        probs_t = work[:, 8192:9216]
        v_diag = work[:, 9216:10240]
        q_diag = work[:, 10240:11264]
        qkv_tok = work[:, 11264:12032]
        k_diag = work[:, 12032:13056]
        v_head = work[:, 13056:13312]
        mask_half = work[:, 13312:14336]
        bias_half = work[:, 14336:15360]
        w_raw = probs
        proj_raw = work[:, 8192:9728]
        proj_sum = qkv_tok
        cen_raw = work[0:NCL, 14336:15360]
        assign_int = work[0:NCL, 7168:8192].bitcast(I32)
        onehot = work[0:NCL, 8192:9216]

        proj_bias = sb("proj_bias", [P, PROJ])
        q_head = sb("q_head", [P, HKV * D])
        own_t = sb("own_t", [P, T4])
        ffn_part = sb("ffn_part", [P, 2, HALF])
        o_head = sb("o_head", [P, HKV * D])
        o_tok = sb("o_tok", [P, HKV * D])
        ident = sb("ident", [P, P])
        ones = sb("ones", [P, P])
        minus_half = sb("minus_half", [P, 1])
        minus_one = sb("minus_one", [P, 1])
        cluster_id = sb("cluster_id", [NCL, 1])
        cluster_int = sb("cluster_int", [NCL, 1], I32)
        cluster_on = sb("cluster_on", [NCL, P])
        hit = sb("hit", [P, NCL])
        best = [sb(f"best{n}", [P, NCL]) for n in range(2)]
        bn = [sb(f"bn{n}", [P, 2, 6]) for n in range(2)]
        moments = [sb(f"moments{n}", [P, 2]) for n in range(2)]
        var_eps = [sb(f"var_eps{n}", [P, 1]) for n in range(2)]
        minus_mean = [sb(f"minus_mean{n}", [P, 1]) for n in range(2)]
        norm = [sb(f"norm{n}", [P, 2]) for n in range(2)]
        norms = [sb(f"norms{n}", [P, NT, 2]) for n in range(2)]
        token_on = [sb(f"token_on{n}", [P, NT]) for n in range(2)]
        neg_max = sb("neg_max", [P, 1])
        exp_bias = sb("exp_bias", [P, 1])
        logit_c = sb("logit_c", [P, NCL])
        exp_c = sb("exp_c", [P, NCL])
        prob_c = sb("prob_c", [P, NCL])
        exp_sum = sb("exp_sum", [P, 1])
        exp_inv = sb("exp_inv", [P, 1])
        prob_max = sb("prob_max", [P, 1])
        row_max = sb("row_max", [P, HEADS])
        row_sum = sb("row_sum", [P, HEADS])
        row_inv = sb("row_inv", [P, HEADS])

        ps_t = ctx.enter_context(nc.psum_tensor("ps_t", [P, KB, P], F32))
        ps_a = ctx.enter_context(nc.psum_tensor("ps_a", [P, 2 * HALF], F32))
        ps_b = ctx.enter_context(nc.psum_tensor("ps_b", [P, 2 * HALF], F32))
        ps_s = ctx.enter_context(nc.psum_tensor("ps_s", [P, 2 * HALF], F32))

        def slot(t):
            return x_ring[:, ds(t % SLOTS, 1), :].rearrange("p a n -> p (a n)")

        def wait(eng, semaphore, value):
            if not isinstance(value, int) or value > 0:
                eng.wait_ge(semaphore, value)

        held = sem("held")

        def wait_alone(eng, semaphore, value):
            eng.wait_ge(semaphore, value)
            eng.sem_inc(held, 1)

        def product(pe, acc, hi, lo, w_h, w_l, cols):
            for k in range(KB):
                pe.matmul(acc, hi[:, k, :], w_h[:, k, cols], start=(k == 0), stop=False)
                pe.matmul(acc, hi[:, k, :], w_l[:, k, cols], start=False, stop=False)
                last = pe.matmul(acc, lo[:, k, :], w_h[:, k, cols], start=False, stop=(k == KB - 1))
            return last

        def transposes(pe, src):
            for k in range(KB):
                last = pe.transpose(ps_t[:, k, :], src[:, k * P:(k + 1) * P], ident[:, :])
            return last

        def clusters(pe, acc, hi, lo):
            for k in range(KB):
                pe.matmul(acc, hi[:, k, :], cen[:, k, :], start=(k == 0), stop=False)
                last = pe.matmul(acc[:, 0:NCL], lo[:, k, :], cen[:, k, 0:NCL], start=False, stop=(k == KB - 1))
            return last

        def layer_norm_stats(dve, x, n, step, t, var_ready, norm_ready):
            dve.bn_stats(bn[n][:, 0, :], x[:, 0:HALF])
            dve.bn_stats(bn[n][:, 1, :], x[:, HALF:EMB]).then_inc(step, 1)
            wait(dve, norm_ready, t)
            wait_alone(dve, step, 2 * t + 1)
            dve.bn_aggr(moments[n][:, :], bn[n][:, :, :]).then_inc(step, 1)
            dve.wait_ge(step, 2 * t + 2)
            dve.tensor_scalar_add(var_eps[n][:, :], moments[n][:, 1:2], EPS).then_inc(var_ready, 1)

        def layer_norm_factors(pool, n, t, var_ready, step, norm_ready, used, saved):
            wait(pool, used, t)
            if saved is not None:
                wait(pool, saved, t)
            pool.wait_ge(var_ready, t + 1)
            pool.tensor_tensor(minus_mean[n][:, :], moments[n][:, 0:1], minus_one[:, :], ALU.mult)
            pool.tensor_tensor(norm[n][:, 1:2], var_eps[n][:, :], minus_half[:, :], ALU.pow).then_inc(step, 1)
            pool.wait_ge(step, t + 1)
            pool.tensor_tensor(norm[n][:, 0:1], minus_mean[n][:, :], norm[n][:, 1:2], ALU.mult).then_inc(norm_ready, 1)
            if saved is not None:
                wait_alone(pool, norm_ready, t + 1)
                pool.tensor_copy(norms[n][:, ds(t, 1), :].rearrange("p a b -> p (a b)"),
                                 norm[n][:, :]).then_inc(saved, 1)

        def saved_norm(n, t):
            pair = norms[n][:, ds(t, 1), :].rearrange("p a b -> p (a b)")
            return pair[:, 0:1], pair[:, 1:2]

        def normed(act, y, x, minus_mean_rstd, rstd):
            return act.activation(y, x, ACT.Identity, bias=minus_mean_rstd, scale=rstd)

        def cluster_max(dve, acc, step, t, acc_read, ready):
            dve.tensor_reduce(logit_c[:, :], acc.rearrange("p (s c) -> p c s", s=2), axis=AX.X,
                              op=ALU.add).then_inc(acc_read, 1)
            dve.wait_ge(acc_read, t + 1)
            dve.tensor_reduce(neg_max[:, :], logit_c[:, :], axis=AX.X, op=ALU.max, negate=True).then_inc(step, 1)
            dve.wait_ge(step, 4 * t + 1)
            dve.tensor_scalar_mul(exp_bias[:, :], neg_max[:, :], INV_TEMPERATURE).then_inc(ready, 1)

        def cluster_exp(act):
            return act.activation(exp_c[:, :], logit_c[:, :], ACT.Exp, bias=exp_bias[:, :],
                                  scale=INV_TEMPERATURE, accum_out=exp_sum[:, :])

        def cluster_probs(dve, n, step, t):
            dve.reciprocal(exp_inv[:, :], exp_sum[:, :]).then_inc(step, 1)
            dve.wait_ge(step, 4 * t + 2)
            dve.tensor_scalar(prob_c[:, :], exp_c[:, :], exp_inv[:, :], None, ALU.mult).then_inc(step, 1)
            dve.wait_ge(step, 4 * t + 3)
            dve.reduce_max(prob_max[:, :], prob_c[:, :], AX.X).then_inc(step, 1)
            dve.tensor_tensor(best[n][:, :], best[n][:, :], prob_c[:, :], ALU.max)
            dve.wait_ge(step, 4 * t + 4)
            dve.tensor_scalar(token_on[n][:, ds(t, 1)], prob_max[:, :], THRESHOLD, None, ALU.is_gt)

        const_set, ident_set, cen_loaded = sem("const_set"), sem("ident_set"), sem("cen_loaded")
        cen_t, cen_hi, cen_lo = sem("cen_t"), sem("cen_hi"), sem("cen_lo")
        w_loaded, wt_done, wt_hi, wt_lo = sem("w_loaded"), sem("wt_done"), sem("wt_hi"), sem("wt_lo")
        raw_loaded, q_summed, kv_moved = sem("raw_loaded"), sem("q_summed"), sem("kv_moved")
        proj_hi_set, proj_lo_set = sem("proj_hi_set"), sem("proj_lo_set")
        s_x_loaded = [sem(f"s_x_loaded{n}") for n in range(2)]
        s_step, s_var, s_power, s_norm = sem("s_step"), sem("s_var"), sem("s_power"), sem("s_norm")
        s_saved = sem("s_saved")
        s_y, s_t, s_hi, s_lo = sem("s_y"), sem("s_t"), sem("s_hi"), sem("s_lo")
        s_c, s_cstep, s_cread, s_cmax, s_cexp = (sem("s_c"), sem("s_cstep"), sem("s_cread"), sem("s_cmax"),
                                                 sem("s_cexp"))
        HD = HKV * D

        def scan(eng, step, block):
            def within(t):
                return 0 <= t < NT
            for i in (-1, 0, 1, 2):
                step(i, i % 2, within, 0)
            block(0, 2)
            with eng.Fori(0, KB - 1) as m:
                for u in range(4):
                    step(m * 4 + (3 + u), (3 + u) % 2, lambda t: True, m + 1 if u == 0 else 0)
                block(m + 1, m * 4 + 6)
            for i in (NT - 1, NT):
                step(i, i % 2, within, KB if i == NT - 1 else 0)

        def scan_slot(t):
            return x_ring[:, ds(t % 4, 1), :].rearrange("p a n -> p (a n)")

        with nc.Block() as block:
            @block.sync
            def _(sp):
                def step(i, par, ok, blocks=0):
                    if ok(i + 4):
                        t, n = i + 4, par
                        if not isinstance(t, int) or t >= 4:
                            wait_alone(sp, s_x_loaded[n], (t - n) * 8)
                            sp.wait_ge(s_y, t - 3)
                        sp.dma_start(scan_slot(t), x_d[ds(t, 1)].rearrange("a p n -> (a p) n")
                                     ).then_inc(s_x_loaded[n], 16)

                def weights(k, srcs):
                    if not isinstance(k, int) or k > 0:
                        wait_alone(sp, q_summed, k)
                        wait_alone(sp, kv_moved, k)
                    wait(sp, raw_loaded, 48 * k)
                    for src, a, b in zip(srcs, (0, EMB, EMB + HD), (EMB, EMB + HD, EMB + 2 * HD)):
                        sp.dma_start(proj_raw[:, a:b], src).then_inc(raw_loaded, 16)

                def block(k, i):
                    k = k + 1
                    wait_alone(sp, wt_done, k)
                    wait(sp, w_loaded, 16 * k)
                    sp.dma_start(w_raw, W[ds(k * P, P), :]).then_inc(w_loaded, 16)
                    weights(k, [w[ds(k * P, P)].rearrange("p d h -> p (d h)") for w in (Wq, Wk, Wv)])

                def within(t):
                    return 0 <= t < NT
                sp.dma_start(cen_raw, centroids).then_inc(cen_loaded, 16)
                for t in range(3):
                    sp.dma_start(scan_slot(t), x_d[t]).then_inc(s_x_loaded[t % 2], 16)
                    if t == 1:
                        sp.wait_ge(s_x_loaded[0], 16)
                sp.dma_start(w_raw, W[0:P, :]).then_inc(w_loaded, 16)
                weights(0, [w[0:P].rearrange("p d h -> p (d h)") for w in (Wq, Wk, Wv)])
                sp.wait_ge(s_x_loaded[1], 16)
                sp.dma_start(scan_slot(3), x_d[3]).then_inc(s_x_loaded[1], 16)
                for i in (0, 1, 2):
                    step(i, i % 2, within)
                block(0, 2)
                with sp.Fori(0, KB - 2) as m:
                    for u in range(4):
                        step(m * 4 + (3 + u), (3 + u) % 2, lambda t: True)
                    block(m + 1, m * 4 + 6)
                step(NT - 5, (NT - 5) % 2, within)
                weights(KB, [b.rearrange("d h -> (d h)").partition_broadcast(P) for b in (bq, bk, bv)])

            @block.gpsimd
            def _(pool):
                pool.memset(ident[:, :], 0.0).then_inc(ident_set, 1)
                pool.memset(ones[:, :], 1.0)
                pool.memset(minus_half[:, :], -0.5)
                pool.memset(minus_one[:, :], -1.0)
                pool.iota(cluster_int[:, :], pattern=[[0, 1]], base=0, channel_multiplier=1).then_inc(const_set, 1)
                pool.wait_ge(ident_set, 1)
                pool.affine_select(out=ident[:, :], in_=ident[:, :], compare_op=ALU.not_equal, fill=1.0, base=0,
                                   pattern=[[-1, P]], channel_multiplier=1).then_inc(ident_set, 1)
                pool.wait_ge(const_set, 1)

                def step(i, par, ok, blocks):
                    if ok(i + 1):
                        layer_norm_factors(pool, 0, i + 1, s_var, s_power, s_norm, s_y, s_saved)

                def block(k, i):
                    pool.wait_ge(proj_hi_set, k + 1)
                    pool.tensor_tensor(proj_lo[:, ds(k, 1), :].rearrange("p a n -> p (a n)"), proj_sum,
                                       proj_hi[:, ds(k, 1), :].rearrange("p a n -> p (a n)").bitcast(F32),
                                       ALU.subtract).then_inc(proj_lo_set, 1)
                scan(pool, step, block)

            @block.scalar
            def _(act):
                act.wait_ge(cen_t, 1)
                act.copy(cen[:, :, 0:NCL], ps_t[:, :, 0:NCL]).then_inc(cen_hi, 1)

                def step(i, par, ok, blocks):
                    if ok(i):
                        act.wait_ge(s_t, i + 1)
                        wait(act, s_c, i - 1)
                        act.copy(y_hi[par][:, :, :], ps_t[:, :, :]).then_inc(s_hi, 1)
                    if ok(i + 1):
                        t, n = i + 1, (par + 1) % 2
                        act.wait_ge(s_norm, t + 1)
                        wait(act, s_t, t - 1)
                        normed(act, y_tok[n], scan_slot(t), norm[0][:, 0:1], norm[0][:, 1:2]).then_inc(s_y, 1)
                    if ok(i - 1):
                        act.wait_ge(s_cmax, i)
                        cluster_exp(act).then_inc(s_cexp, 1)

                def move_kv(k, dst):
                    act.wait_ge(raw_loaded, 48 * k + 48)
                    for a, b in ((EMB, HD), (EMB + HD, 2 * HD)):
                        moved = act.copy(dst[:, b:b + HD].rearrange("p (g d) -> p d g", g=HKV),
                                         proj_raw[:, a:a + HD].rearrange("p (d g) -> p d g", g=HKV))
                    moved.then_inc(kv_moved, 1)

                def block(k, i):
                    act.wait_ge(wt_done, k + 1)
                    act.copy(w_hi[:, :, ds(k * P, P)], ps_t[:, :, :]).then_inc(wt_hi, 1)
                    wait(act, proj_lo_set, k)
                    move_kv(k, proj_sum)
                    act.wait_ge(q_summed, k + 1)
                    act.wait_ge(kv_moved, k + 1)
                    act.copy(proj_hi[:, ds(k, 1), :].rearrange("p a n -> p (a n)"), proj_sum).then_inc(proj_hi_set, 1)
                scan(act, step, block)
                move_kv(KB, proj_bias)

            @block.vector
            def _(dve):
                dve.memset(best[0][:, :], 0.0)
                dve.memset(best[1][:, :], 0.0)
                dve.wait_ge(ident_set, 2)
                dve.reduce_sum(own_t[:, :], ident[:, :].rearrange("p (c t) -> p t c", t=T4), AX.X)
                dve.wait_ge(const_set, 1)
                dve.tensor_copy(cluster_id[:, :], cluster_int[:, :])
                dve.wait_ge(cen_hi, 1)
                dve.tensor_tensor(cen[:, :, NCL:2 * NCL], ps_t[:, :, 0:NCL], cen[:, :, 0:NCL].bitcast(F32),
                                  ALU.subtract).then_inc(cen_lo, 1)

                def step(i, par, ok, blocks):
                    if ok(i + 1):
                        t, n = i + 1, (par + 1) % 2
                        dve.wait_ge(s_x_loaded[n], (t - n) * 8 + 16)
                        layer_norm_stats(dve, scan_slot(t), 0, s_step, t, s_var, s_norm)
                    if ok(i):
                        dve.wait_ge(s_hi, i + 1)
                        dve.tensor_tensor(y_lo[par][:, :, :], ps_t[:, :, :], y_hi[par][:, :, :].bitcast(F32),
                                          ALU.subtract).then_inc(s_lo, 1)
                    if ok(i - 1):
                        t, n = i - 1, (par + 1) % 2
                        dve.wait_ge(s_c, t + 1)
                        cluster_max(dve, (ps_a, ps_b)[n][:, 0:2 * NCL], s_cstep, t, s_cread, s_cmax)
                        dve.wait_ge(s_cexp, t + 1)
                        cluster_probs(dve, 0, s_cstep, t)

                def sum_q(k, dst):
                    dve.wait_ge(raw_loaded, 48 * k + 48)
                    dve.tensor_reduce(dst[:, 0:HD].rearrange("p (g d) -> p g d", g=HKV),
                                      proj_raw[:, 0:EMB].rearrange("p (d g r) -> p g d r", g=HKV, r=SCALE),
                                      axis=AX.X, op=ALU.add).then_inc(q_summed, 1)

                def block(k, i):
                    wait(dve, proj_lo_set, k)
                    sum_q(k, proj_sum)
                    dve.wait_ge(wt_hi, k + 1)
                    dve.tensor_tensor(w_lo[:, :, ds(k * P, P)], ps_t[:, :, :], w_hi[:, :, ds(k * P, P)].bitcast(F32),
                                      ALU.subtract).then_inc(wt_lo, 1)
                scan(dve, step, block)
                sum_q(KB, proj_bias)

            @block.tensor
            def _(pe):
                pe.wait_ge(ident_set, 2)
                pe.wait_ge(cen_loaded, 16)
                for k in range(KB):
                    last = pe.transpose(ps_t[:, k, 0:NCL], cen_raw[:, k * P:(k + 1) * P], ident[0:NCL, 0:NCL])
                last.then_inc(cen_t, 1)
                pe.wait_ge(cen_lo, 1)

                def step(i, par, ok, blocks):
                    if ok(i):
                        pe.wait_ge(s_y, i + 1)
                        wait(pe, s_lo, i)
                        wait(pe, wt_lo, blocks)
                        transposes(pe, y_tok[par]).then_inc(s_t, 1)
                    if ok(i - 1):
                        t, n = i - 1, (par + 1) % 2
                        pe.wait_ge(s_lo, t + 1)
                        wait(pe, s_cread, t - 1)
                        clusters(pe, (ps_a, ps_b)[n][:, 0:2 * NCL], y_hi[n], y_lo[n]).then_inc(s_c, 1)

                def block(k, i):
                    pe.wait_ge(w_loaded, 16 * k + 16)
                    pe.wait_ge(s_lo, i + 1)
                    transposes(pe, w_raw).then_inc(wt_done, 1)
                scan(pe, step, block)

        def select(n):
            m_bias, m_assign = sem(f"m_bias{n}"), sem(f"m_assign{n}")
            m_hit, m_count, m_on, m_step = (sem(f"m_hit{n}"), sem(f"m_count{n}"), sem(f"m_on{n}"),
                                            sem(f"m_step{n}"))
            m_rows, m_mask = sem(f"m_rows{n}"), sem(f"m_mask{n}")
            with nc.Block() as block:
                @block.sync
                def _(sp):
                    sp.dma_start(assign_int, assignments.partition_broadcast(NCL)).then_inc(m_assign, 16)
                    sp.dma_start(bias_half, ffn_bias.partition_broadcast(P)).then_inc(m_bias, 16)

                @block.gpsimd
                def _(pool):
                    if n == 0:
                        pool.memset(v_diag, 0.0)
                        pool.memset(k_diag, 0.0)

                @block.vector
                def _(dve):
                    dve.tensor_scalar(hit[:, :], best[n][:, :], THRESHOLD, None, ALU.is_gt).then_inc(m_hit, 1)
                    dve.wait_ge(m_assign, 16)
                    dve.tensor_copy(onehot, assign_int).then_inc(m_step, 1)
                    dve.wait_ge(m_step, 1)
                    dve.tensor_scalar(onehot, onehot, cluster_id[:, :], None, ALU.is_equal).then_inc(m_step, 1)
                    dve.wait_ge(m_count, 1)
                    dve.tensor_scalar(cluster_on[:, :], ps_b[0:NCL, 0:P], 1.0, 0.5, ALU.min, ALU.mult).then_inc(m_on, 1)
                    dve.wait_ge(m_rows, 1)
                    dve.tensor_copy(mask_half, ps_a[:, :]).then_inc(m_mask, 1)
                    dve.wait_ge(m_mask, 1)
                    dve.wait_ge(m_bias, 16)
                    dve.tensor_tensor(bias_half, bias_half, mask_half, ALU.mult)

                @block.tensor
                def _(pe):
                    pe.wait_ge(m_hit, 1)
                    pe.matmul(ps_b[0:NCL, 0:P], hit[:, :], ones[:, :], start=True, stop=True).then_inc(m_count, 1)
                    pe.wait_ge(m_on, 1)
                    pe.wait_ge(m_step, 2)
                    for h in range(2):
                        last = pe.matmul(ps_a[:, h * HALF:(h + 1) * HALF], cluster_on[:, :],
                                         onehot[:, h * HALF:(h + 1) * HALF], start=True, stop=True)
                    last.then_inc(m_rows, 1)

        select(0)

        x_loaded, x2_ready, x2_stored = sem("x_loaded"), sem("x2_ready"), sem("x2_stored")
        y1_ready, y2_ready, y3_ready = sem("y1_ready"), sem("y2_ready"), sem("y3_ready")
        t1_done, t2_done, t3_done = sem("t1_done"), sem("t2_done"), sem("t3_done")
        hi1, hi2, hi3 = sem("hi1"), sem("hi2"), sem("hi3")
        lo1, lo2, lo3 = sem("lo1"), sem("lo2"), sem("lo3")
        ffn_done, ffn_read, x1_step = sem("ffn_done"), sem("ffn_read"), sem("x1_step")
        ln2_step, var2, power2, norm2 = sem("ln2_step"), sem("var2"), sem("power2"), sem("norm2")
        saved3 = sem("saved3")
        ln3_step, var3, power3, norm3 = sem("ln3_step"), sem("var3"), sem("power3"), sem("norm3")
        proj_done, proj_read, qkv_stored = sem("proj_done"), sem("proj_read"), sem("qkv_stored")
        q_loaded, k_loaded, v_loaded = sem("q_loaded"), sem("k_loaded"), sem("v_loaded")
        q_diag_ready, v_diag_ready = sem("q_diag_ready"), sem("v_diag_ready")
        scores_done, scores_read, exp_ready = sem("scores_done"), sem("scores_read"), sem("exp_ready")
        soft_step, probs_ready, heads_done = sem("soft_step"), sem("probs_ready"), sem("heads_done")
        o_ready, o_stored, o_loaded = sem("o_ready"), sem("o_stored"), sem("o_loaded")
        c_done, c_step, c_read, c_max, c_exp = sem("c_done"), sem("c_step"), sem("c_read"), sem("c_max"), sem("c_exp")

        def main(eng, emit):
            for i in range(-1, 4):
                emit(i, lambda t: 0 <= t < NT)
            with eng.Fori(4, NT - 2) as i:
                emit(i, lambda t: True)
            for i in range(NT - 2, NT + 3):
                emit(i, lambda t: 0 <= t < NT)

        def prob_block(r, j):
            return (j * R4 + r) * D

        with nc.Block() as block:
            @block.sync
            def _(sp):
                def load(t):
                    wait(sp, x_loaded, 16 * t)
                    sp.dma_start(slot(t), x_d[ds(t, 1)].rearrange("a p n -> (a p) n")).then_inc(x_loaded, 16)

                def step(i, ok):
                    if ok(i - 3):
                        t = i - 3
                        sp.wait_ge(x2_ready, t + 1)
                        sp.dma_start(x2_d[ds(t, 1)].rearrange("a p n -> (a p) n"), slot(t)).then_inc(x2_stored, 16)
                    if ok(i + 2):
                        if ok(i - 3):
                            sp.wait_ge(x2_stored, 16 * (i - 2))
                            sp.wait_ge(y3_ready, i - 2)
                        load(i + 2)
                    if ok(i - 1):
                        t = i - 1
                        sp.wait_ge(proj_read, 2 * t + 2)
                        sp.dma_start(qkv_d[ds(t, 1)].rearrange("a s k e -> (a k) s e"),
                                     qkv_tok.rearrange("p (s e) -> p s e", e=D)).then_inc(qkv_stored, 16)
                    if ok(i - 2):
                        t = i - 2
                        sp.wait_ge(o_stored, 16 * t + 16)
                        wait(sp, x2_ready, t)
                        sp.dma_start(o_tok[:, :].rearrange("p (g d) -> p g d", g=HKV),
                                     o_d[ds(t, 1)].rearrange("a g k d -> (a k) g d")).then_inc(o_loaded, 16)
                    if ok(i - 1):
                        t = i - 1
                        sp.wait_ge(qkv_stored, 16 * t + 16)
                        q, k, v = (qkv_d[ds(t, 1), HKV * s:HKV * (s + 1)] for s in range(3))
                        by_row_block = "a g (t r j) e -> r (a g t) (j e)"
                        wait(sp, q_diag_ready, t)
                        sp.dma_start(q_head[:, :], q.rearrange(by_row_block, t=T4, r=R4)).then_inc(q_loaded, 16)
                        wait(sp, scores_done, t)
                        for r in range(R4):
                            sp.dma_start(k_diag[32 * r:32 * r + 32, r * J8 * D:(r + 1) * J8 * D],
                                         k.rearrange(by_row_block, t=T4, r=R4)[r]).then_inc(k_loaded, 16)
                        wait(sp, v_diag_ready, t)
                        sp.dma_start(v_head, v.rearrange("a g (n j) e -> (a n) g (j e)", j=J8)).then_inc(v_loaded, 16)
                load(0)
                main(sp, step)
                sp.wait_ge(x2_stored, 16 * NT)

            @block.gpsimd
            def _(pool):
                def step(i, ok):
                    if ok(i - 3):
                        layer_norm_factors(pool, 1, i - 3, var3, power3, norm3, y3_ready, saved3)
                    if ok(i):
                        layer_norm_factors(pool, 0, i, var2, power2, norm2, y2_ready, None)
                main(pool, step)

            @block.scalar
            def _(act):
                def step(i, ok):
                    if ok(i + 1):
                        t = i + 1
                        act.wait_ge(x_loaded, 16 * t + 16)
                        wait(act, t2_done, i)
                        normed(act, y_tok[0], slot(t), *saved_norm(0, t)).then_inc(y1_ready, 1)
                    if ok(i - 2):
                        t = i - 2
                        act.wait_ge(q_loaded, 16 * t + 16)
                        wait(act, scores_done, t)
                        for b in range(T4):
                            last = act.activation(q_diag.rearrange("p (j t d) -> p j t d", t=T4, d=D)[:, :, b, :],
                                                  q_head[:, :].rearrange("p (j d) -> p j d", d=D), ACT.Identity,
                                                  scale=own_t[:, b:b + 1])
                        last.then_inc(q_diag_ready, 1)
                    if ok(i - 3):
                        t = i - 3
                        act.wait_ge(norm3, t + 1)
                        wait(act, t3_done, t)
                        normed(act, y_tok[1], slot(t), norm[1][:, 0:1], norm[1][:, 1:2]).then_inc(y3_ready, 1)
                        act.wait_ge(t3_done, t + 1)
                        act.copy(y_hi[0][:, :, :], ps_t[:, :, :]).then_inc(hi3, 1)
                    if ok(i - 2):
                        act.wait_ge(scores_read, i - 1)
                        act.activation(probs, probs, ACT.Exp, scale=1.0 / float(np.sqrt(D))).then_inc(exp_ready, 1)
                    if ok(i + 1):
                        act.wait_ge(t1_done, i + 2)
                        act.copy(y_hi[0][:, :, :], ps_t[:, :, :]).then_inc(hi1, 1)
                    if ok(i):
                        act.wait_ge(norm2, i + 1)
                        act.wait_ge(t1_done, i + 2 if ok(i + 1) else NT)
                        normed(act, y_tok[0], slot(i), norm[0][:, 0:1], norm[0][:, 1:2]).then_inc(y2_ready, 1)
                    if ok(i - 2):
                        act.wait_ge(heads_done, i - 1)
                        wait(act, o_stored, 16 * (i - 2))
                        act.copy(o_head[:, :], ps_s[:, 0:HKV * D]).then_inc(o_ready, 1)
                        act.wait_ge(o_ready, i - 1)
                        act.dma_start(o_d[ds(i - 2, 1)].rearrange("a g (t r j) d -> r (a g t) (j d)", t=T4, r=R4),
                                      o_head[:, :]).then_inc(o_stored, 16)
                    if ok(i - 3):
                        act.wait_ge(c_max, i - 2)
                        cluster_exp(act).then_inc(c_exp, 1)
                    if ok(i):
                        act.wait_ge(t2_done, i + 1)
                        act.copy(y_hi[1][:, :, :], ps_t[:, :, :]).then_inc(hi2, 1)
                main(act, step)

            @block.vector
            def _(dve):
                def low_part(n, hi_sem, lo_sem, t):
                    dve.wait_ge(hi_sem, t + 1)
                    dve.tensor_tensor(y_lo[n][:, :, :], ps_t[:, :, :], y_hi[n][:, :, :].bitcast(F32),
                                      ALU.subtract).then_inc(lo_sem, 1)

                def ffn_half(i, n):
                    h = 1 - n
                    cols = slice(h * HALF, (h + 1) * HALF)
                    dve.wait_ge(ffn_done, 2 * i + n + 1)
                    dve.scalar_tensor_tensor(ffn_part[:, n, :], ps_a[:, cols], token_on[0][:, ds(i, 1)],
                                             mask_half[:, cols], ALU.mult, ALU.mult).then_inc(ffn_read, 1)
                    dve.wait_ge(ffn_read, 2 * i + n + 1)
                    dve.tensor_tensor(slot(i)[:, cols], slot(i)[:, cols], ffn_part[:, n, :],
                                      ALU.add).then_inc(x1_step, 1)

                def step(i, ok):
                    if ok(i):
                        dve.wait_ge(x_loaded, 16 * i + 16)
                        dve.wait_ge(y1_ready, i + 1)
                        dve.scalar_tensor_tensor(slot(i), bias_half, token_on[0][:, ds(i, 1)], slot(i), ALU.mult,
                                                 ALU.add).then_inc(x1_step, 1)
                    if ok(i - 3):
                        t = i - 3
                        dve.wait_ge(o_loaded, 16 * t + 16)
                        dve.wait_ge(y2_ready, t + 1)
                        x2 = slot(t)
                        x2_v = x2.rearrange("p (d g r) -> p d g r", g=HKV, r=SCALE)
                        o_v = o_tok[:, :].rearrange("p (g d) -> p d g", g=HKV).unsqueeze(3).to_broadcast([P, D, HKV, SCALE])
                        dve.tensor_tensor(x2_v, x2_v, o_v, ALU.add).then_inc(x2_ready, 1)
                        wait_alone(dve, x2_ready, t + 1)
                        layer_norm_stats(dve, x2, 1, ln3_step, t, var3, norm3)
                    if ok(i):
                        dve.wait_ge(x1_step, 3 * i + 1)
                        ffn_half(i, 0)
                    if ok(i - 2):
                        t = i - 2
                        dve.wait_ge(v_loaded, 16 * t + 16)
                        wait(dve, heads_done, t)
                        for b in range(T4):
                            last = dve.transpose(v_diag[32 * b:32 * b + 32, b:EMB:T4], v_head[32 * b:32 * b + 32, :])
                        last.then_inc(v_diag_ready, 1)
                    if ok(i):
                        ffn_half(i, 1)
                        wait_alone(dve, x1_step, 3 * i + 3)
                        layer_norm_stats(dve, slot(i), 0, ln2_step, i, var2, norm2)
                    if ok(i - 2):
                        t = i - 2
                        groups = "p (c e) -> p c e"
                        wide = [P, HEADS, D]
                        probs_v = probs.rearrange(groups, e=D)
                        scores_v = ps_s[:, :].rearrange(groups, e=D)
                        dve.wait_ge(scores_done, t + 1)
                        dve.reduce_max(row_max[:, :], scores_v, AX.X).then_inc(soft_step, 1)
                        dve.wait_ge(soft_step, 4 * t + 1)
                        dve.tensor_tensor(probs_v, scores_v, row_max[:, :].unsqueeze(2).to_broadcast(wide),
                                          ALU.subtract).then_inc(scores_read, 1)
                    if ok(i - 3):
                        low_part(0, hi3, lo3, i - 3)
                    if ok(i - 2):
                        dve.wait_ge(exp_ready, t + 1)
                        dve.reduce_sum(row_sum[:, :], probs_v, AX.X).then_inc(soft_step, 1)
                    if ok(i - 2):
                        dve.wait_ge(soft_step, 4 * t + 2)
                        dve.reciprocal(row_inv[:, :], row_sum[:, :]).then_inc(soft_step, 1)
                        dve.wait_ge(soft_step, 4 * t + 3)
                        dve.tensor_tensor(probs_v, probs_v, row_inv[:, :].unsqueeze(2).to_broadcast(wide),
                                          ALU.mult).then_inc(soft_step, 1)
                        dve.wait_ge(soft_step, 4 * t + 4)
                        wait(dve, heads_done, t)
                        dve.transpose(probs_t, probs).then_inc(probs_ready, 1)
                    if ok(i + 1):
                        low_part(0, hi1, lo1, i + 1)
                    if ok(i - 3):
                        dve.wait_ge(c_done, i - 2)
                        cluster_max(dve, ps_a[:, 0:2 * NCL], c_step, i - 3, c_read, c_max)
                    if ok(i - 1):
                        t = i - 1
                        wait(dve, qkv_stored, 16 * t)
                        for n, cols in enumerate((slice(0, HALF), slice(HALF, PROJ))):
                            dve.wait_ge(proj_done, 2 * t + n + 1)
                            dve.tensor_tensor(qkv_tok[:, cols], ps_b[:, cols], proj_bias[:, cols],
                                              ALU.add).then_inc(proj_read, 1)
                    if ok(i):
                        low_part(1, hi2, lo2, i)
                    if ok(i - 3):
                        dve.wait_ge(c_exp, i - 2)
                        cluster_probs(dve, 1, c_step, i - 3)
                main(dve, step)

            @block.tensor
            def _(pe):
                def projection(t, cols):
                    pe.wait_ge(lo2, t + 1)
                    wait(pe, proj_read, 2 * t)
                    product(pe, ps_b[:, cols], y_hi[1], y_lo[1], proj_hi, proj_lo, cols).then_inc(proj_done, 1)

                def step(i, ok):
                    if ok(i):
                        pe.wait_ge(lo1, i + 1)
                        wait(pe, ffn_read, 2 * i)
                        product(pe, ps_a[:, HALF:EMB], y_hi[0], y_lo[0], w_hi, w_lo,
                                slice(HALF, EMB)).then_inc(ffn_done, 1)
                        if ok(i - 4):
                            pe.wait_ge(c_read, i - 3)
                        product(pe, ps_a[:, 0:HALF], y_hi[0], y_lo[0], w_hi, w_lo,
                                slice(0, HALF)).then_inc(ffn_done, 1)
                    if ok(i - 3):
                        pe.wait_ge(y3_ready, i - 2)
                        pe.wait_ge(lo2, i if ok(i) else NT)
                        transposes(pe, y_tok[1]).then_inc(t3_done, 1)
                    if ok(i - 2):
                        t = i - 2
                        pe.wait_ge(q_diag_ready, t + 1)
                        pe.wait_ge(k_loaded, 16 * R4 * (t + 1))
                        wait(pe, o_ready, t)
                        k_blocks = k_diag.rearrange("p (r j e) -> p j r e", r=R4, e=D)
                        for j in range(J8):
                            last = pe.matmul(ps_s[:, j * P:(j + 1) * P], q_diag[:, j * P:(j + 1) * P],
                                             k_blocks[:, j, :, :], start=True, stop=True)
                        last.then_inc(scores_done, 1)
                    if ok(i - 1):
                        projection(i - 1, slice(0, HALF))
                    if ok(i - 3):
                        pe.wait_ge(lo3, i - 2)
                        pe.wait_ge(ffn_read, 2 * i + 2 if ok(i) else 2 * NT)
                        clusters(pe, ps_a[:, 0:2 * NCL], y_hi[0], y_lo[0]).then_inc(c_done, 1)
                    if ok(i + 1):
                        pe.wait_ge(y1_ready, i + 2)
                        if ok(i - 3):
                            pe.wait_ge(lo3, i - 2)
                        else:
                            wait(pe, lo2, i)
                        transposes(pe, y_tok[0]).then_inc(t1_done, 1)
                    if ok(i - 1):
                        projection(i - 1, slice(HALF, PROJ))
                    if ok(i - 2):
                        t = i - 2
                        pe.wait_ge(probs_ready, t + 1)
                        pe.wait_ge(v_diag_ready, t + 1)
                        for j in range(J8):
                            for r in range(R4):
                                c = prob_block(r, j)
                                last = pe.matmul(ps_s[32 * r:32 * r + 32, j * D:(j + 1) * D],
                                                 v_diag[:, (j * R4 + r) * 32:(j * R4 + r + 1) * 32],
                                                 probs_t[:, c:c + D], start=True, stop=True)
                        last.then_inc(heads_done, 1)
                    if ok(i):
                        pe.wait_ge(y2_ready, i + 1)
                        if ok(i + 1):
                            pe.wait_ge(lo1, i + 2)
                        else:
                            pe.wait_ge(lo3, i - 2)
                        transposes(pe, y_tok[0]).then_inc(t2_done, 1)
                main(pe, step)

        select(1)

        f_x_loaded = [sem(f"f_x_loaded{n}") for n in range(2)]
        f_y, f_t, f_hi, f_lo = sem("f_y"), sem("f_t"), sem("f_hi"), sem("f_lo")
        f_ffn, f_read, f_step, f_out = sem("f_ffn"), sem("f_read"), sem("f_step"), sem("f_out")

        def finish(eng, emit):
            for i in (-2, -1, 0, 1):
                emit(i, i % 2, lambda t: 0 <= t < NT)
            with eng.Fori(1, (NT - 2) // 2) as m:
                for u in range(2):
                    emit(m * 2 + u, u, lambda t: True)
            for i in (NT - 2, NT - 1):
                emit(i, i % 2, lambda t: 0 <= t < NT)

        with nc.Block() as block:
            @block.sync
            def _(sp):
                def load(t, n):
                    wait(sp, f_x_loaded[n], (t - n) * 8)
                    sp.dma_start(slot(t), x2_d[ds(t, 1)].rearrange("a p n -> (a p) n")).then_inc(f_x_loaded[n], 16)

                def step(i, par, ok):
                    if ok(i):
                        wait_alone(sp, f_step, 3 * i + 3)
                        wait(sp, f_out, 16 * i)
                        sp.dma_start(out_d[ds(i, 1)].rearrange("a p n -> (a p) n"), slot(i)).then_inc(f_out, 16)
                    if ok(i + 4):
                        if ok(i - 1):
                            sp.wait_ge(f_out, 16 * i)
                        load(i + 4, par)
                load(0, 0)
                load(1, 1)
                for i in (-2, -1):
                    step(i, i % 2, lambda t: 0 <= t < NT)
                step(0, 0, lambda t: 0 <= t < NT)
                step(1, 1, lambda t: 0 <= t < NT)
                with sp.Fori(1, (NT - 4) // 2) as m:
                    for u in range(2):
                        step(m * 2 + u, u, lambda t: True)
                for i in range(NT - 4, NT):
                    step(i, i % 2, lambda t: 0 <= t < NT)
                sp.wait_ge(f_out, 16 * NT)

            @block.vector
            def _(dve):
                def step(i, par, ok):
                    if ok(i + 1):
                        n = (par + 1) % 2
                        dve.wait_ge(f_hi, i + 2)
                        dve.tensor_tensor(y_lo[n][:, :, :], ps_t[:, :, :], y_hi[n][:, :, :].bitcast(F32),
                                          ALU.subtract).then_inc(f_lo, 1)
                    if ok(i):
                        dve.wait_ge(f_y, i + 1)
                        acc = (ps_a, ps_b)[par]
                        on = token_on[1][:, ds(i, 1)]
                        dve.scalar_tensor_tensor(slot(i), bias_half, on, slot(i), ALU.mult, ALU.add).then_inc(f_step, 1)
                        dve.wait_ge(f_step, 3 * i + 1)
                        for h in range(2):
                            cols = slice(h * HALF, (h + 1) * HALF)
                            dve.wait_ge(f_ffn, 2 * i + h + 1)
                            dve.scalar_tensor_tensor(ffn_part[:, h, :], acc[:, cols], on, mask_half[:, cols],
                                                     ALU.mult, ALU.mult).then_inc(f_read, 1)
                            dve.wait_ge(f_read, 2 * i + h + 1)
                            dve.tensor_tensor(slot(i)[:, cols], slot(i)[:, cols], ffn_part[:, h, :],
                                              ALU.add).then_inc(f_step, 1)
                finish(dve, step)

            @block.scalar
            def _(act):
                def step(i, par, ok):
                    if ok(i + 1):
                        n = (par + 1) % 2
                        act.wait_ge(f_t, i + 2)
                        act.copy(y_hi[n][:, :, :], ps_t[:, :, :]).then_inc(f_hi, 1)
                    if ok(i + 2):
                        t = i + 2
                        act.wait_ge(f_x_loaded[par], (t - par) * 8 + 16)
                        wait(act, f_t, i + 1)
                        normed(act, y_tok[par], slot(t), *saved_norm(1, t)).then_inc(f_y, 1)
                finish(act, step)

            @block.tensor
            def _(pe):
                def step(i, par, ok):
                    if ok(i + 1):
                        n = (par + 1) % 2
                        pe.wait_ge(f_y, i + 2)
                        wait(pe, f_lo, i + 1)
                        transposes(pe, y_tok[n]).then_inc(f_t, 1)
                    if ok(i):
                        pe.wait_ge(f_lo, i + 1)
                        wait(pe, f_read, 2 * (i - 1))
                        for h in range(2):
                            cols = slice(h * HALF, (h + 1) * HALF)
                            product(pe, (ps_a, ps_b)[par][:, cols], y_hi[par], y_lo[par], w_hi, w_lo,
                                    cols).then_inc(f_ffn, 1)
                finish(pe, step)


_INS = ["L0_attn_x", "L0_attn_Wq", "L0_attn_bq", "L0_attn_Wk", "L0_attn_bk", "L0_attn_Wv", "L0_attn_bv",
        "L0_ffn_weight", "L0_ffn_bias", "L0_ffn_centroids", "L0_ffn_assignments"]


def kernel(**inputs):
    import numpy as _np
    import concourse.bacc as _bacc
    from concourse import mybir as _mybir
    from concourse.bass_utils import run_bass_kernel_spmd as _run

    nc = _bacc.Bacc("TRN2", target_bir_lowering=False, num_devices=1)
    arrays, args = {}, []
    for name in _INS:
        a = _np.ascontiguousarray(inputs[name])
        arrays[f"in_{name}"] = a
        args.append(nc.dram_tensor(f"in_{name}", a.shape, _mybir.dt.from_np(a.dtype), kind="ExternalInput").ap())
    shape = arrays["in_L0_attn_x"].shape
    args.append(nc.dram_tensor("out", shape, _mybir.dt.float32, kind="ExternalOutput").ap())
    macaron_kernel(nc, *args)
    r = _run(nc, [arrays], core_ids=[0])
    return r.results[0]["out"]
```

```python
import numpy as np
import concourse.bass as bass
from concourse import mybir
from contextlib import ExitStack

F32 = mybir.dt.float32
F32R = mybir.dt.float32r
BF16 = mybir.dt.bfloat16
I32 = mybir.dt.int32
ALU = mybir.AluOpType
ACT = mybir.ActivationFunctionType
AX = mybir.AxisListType
ds = bass.ds

P = 128
EMB = 1024
KB = EMB // P
HEADS = 32
SCALE = 4
D = EMB // HEADS
HKV = HEADS // SCALE
PROJ = 3 * HKV * D
NCL = 64
THRESHOLD = 0.01
INV_TEMPERATURE = 10.0
EPS = 1e-5
T4, R4, J8 = 4, 4, 8
SLOTS = 5
HALF = 512
GROUP = 4


def macaron_kernel(nc, x_in, Wq, bq, Wk, bk, Wv, bv, W, ffn_bias, centroids, assignments, out):
    x_d = x_in.rearrange("b (n p) e -> (b n) p e", p=P)
    out_d = out.rearrange("b (n p) e -> (b n) p e", p=P)
    NT = x_d.shape[0]

    x2_d = nc.dram_tensor("x2_scratch", (NT, P, EMB), F32, kind="Internal").ap()
    qkv_d = nc.dram_tensor("qkv_scratch", (NT, 3 * HKV, P, D), F32, kind="Internal").ap()
    o_d = nc.dram_tensor("o_scratch", (NT, HKV, P, D), F32, kind="Internal").ap()

    ctx = ExitStack()
    with ctx:
        def sb(name, shape, dt=F32):
            return ctx.enter_context(nc.sbuf_tensor(name, shape, dt))

        def sem(name):
            return ctx.enter_context(nc.semaphore(name))

        w_hi, w_lo = sb("w_hi", [P, KB, EMB], F32R), sb("w_lo", [P, KB, EMB], F32R)
        proj_hi, proj_lo = sb("proj_hi", [P, KB, PROJ], F32R), sb("proj_lo", [P, KB, PROJ], F32R)
        cen = sb("cen", [P, KB, 2 * NCL], F32R)
        y_hi_pair, y_lo_pair = sb("y_hi", [P, KB, 2, P], F32R), sb("y_lo", [P, KB, 2, P], F32R)
        y_hi = [y_hi_pair[:, :, n, :] for n in range(2)]
        y_lo = [y_lo_pair[:, :, n, :] for n in range(2)]

        work = sb("work", [P, 10240])
        x_ring = work[:, 0:SLOTS * EMB].rearrange("p (s n) -> p s n", n=EMB)
        y_tok = [work[:, 5120:6144], work[:, 6144:7168]]
        probs = work[:, 7168:8192]
        probs_t = work[:, 8192:9216]
        v_diag = work[:, 9216:10240]
        w_raw = probs
        proj_raw = work[:, 8192:9728]
        cen_raw = y_tok[1][0:NCL, :]
        assign_int = work[0:NCL, 4096:5120].bitcast(I32)
        assign = y_tok[0][0:NCL, :]
        group_exp_in, group_exp = work[:, 4096:4352], work[:, 4352:4608]
        pair_sums = work[:, 4608:4864]
        fold = work[:, 4864:4928]
        group_best = work[:, 4928:4992]
        group_max, group_sum, group_inv, group_top = (work[:, 4992 + GROUP * n:4992 + GROUP * (n + 1)]
                                                      for n in range(4))
        bias_raw = probs

        proj_bias = sb("proj_bias", [P, PROJ])
        q_head = sb("q_head", [P, HKV * D])
        own_t = sb("own_t", [P, T4])
        ffn_part = sb("ffn_part", [P, 2, HALF])
        o_head = sb("o_head", [P, HKV * D])
        o_tok = sb("o_tok", [P, HKV * D])
        ident = sb("ident", [P, P])
        ones = sb("ones", [P, P])
        minus_half = sb("minus_half", [P, 1])
        minus_one = sb("minus_one", [P, 1])
        eps = sb("eps", [P, 1])
        cluster_id = sb("cluster_id", [NCL, 1])
        cluster_int = sb("cluster_int", [NCL, 1], I32)
        onehot = sb("onehot", [NCL, EMB], BF16)
        best = [sb(f"best{n}", [P, NCL]) for n in range(2)]
        bn = [sb(f"bn{n}", [P, 2, 6]) for n in range(2)]
        moments = [sb(f"moments{n}", [P, 2]) for n in range(2)]
        var_eps = [sb(f"var_eps{n}", [P, 1]) for n in range(2)]
        minus_mean = [sb(f"minus_mean{n}", [P, 1]) for n in range(2)]
        norm = [sb(f"norm{n}", [P, 2]) for n in range(2)]
        norms = [sb(f"norms{n}", [P, NT, 2]) for n in range(2)]
        token_on = [sb(f"token_on{n}", [P, NT]) for n in range(2)]
        neg_max = sb("neg_max", [P, 1])
        exp_bias = sb("exp_bias", [P, 1])
        logit_c = sb("logit_c", [P, NCL])
        hit = logit_c
        exp_c = sb("exp_c", [P, NCL])
        prob_c = exp_c
        exp_sum = sb("exp_sum", [P, 1])
        exp_inv = sb("exp_inv", [P, 1])
        prob_max = sb("prob_max", [P, 1])
        row_max = sb("row_max", [P, HEADS])
        row_sum = sb("row_sum", [P, HEADS])
        row_inv = sb("row_inv", [P, HEADS])

        ps_t = ctx.enter_context(nc.psum_tensor("ps_t", [P, KB, P], F32))
        ps_a = ctx.enter_context(nc.psum_tensor("ps_a", [P, 2 * HALF], F32))
        ps_b = ctx.enter_context(nc.psum_tensor("ps_b", [P, 2 * HALF], F32))
        ps_s = ctx.enter_context(nc.psum_tensor("ps_s", [P, 2 * HALF], F32))

        scan_ps = [ps_t[:, :, :], ps_s[:, :].rearrange("p (k n) -> p k n", n=P)]
        ps_t_flat = ps_t[:, :, :].rearrange("p k n -> p (k n)")
        weight_ps = ps_b[:, :].rearrange("p (k n) -> p k n", n=P)
        pair_ps = ps_a[:, 0:2 * P]
        group_ps = ps_a[:, HALF:HALF + GROUP * NCL]

        scan_memory = ExitStack()
        scan_hi = [y_hi_pair, scan_memory.enter_context(nc.sbuf_tensor("scan_hi", [P, KB, 2, P], F32R))]
        scan_lo = [y_lo_pair, scan_memory.enter_context(nc.sbuf_tensor("scan_lo", [P, KB, 2, P], F32R))]
        proj_sum = scan_memory.enter_context(nc.sbuf_tensor("proj_sum", [P, PROJ], F32))[:, :]

        def slot(t):
            return x_ring[:, ds(t % SLOTS, 1), :].rearrange("p a n -> p (a n)")

        def is_int(i, n):
            return isinstance(i, int) and i == n

        def wait(eng, semaphore, value):
            if not isinstance(value, int) or value > 0:
                eng.wait_ge(semaphore, value)

        held, best_set = sem("held"), sem("best_set")

        def wait_alone(eng, semaphore, value):
            eng.wait_ge(semaphore, value)
            eng.sem_inc(held, 1)

        def product(pe, acc, hi, lo, w_h, w_l, cols, amid=lambda: None):
            for k in range(KB):
                if k == 1:
                    amid()
                pe.matmul(acc, hi[:, k, :], w_h[:, k, cols], start=(k == 0), stop=False)
                pe.matmul(acc, hi[:, k, :], w_l[:, k, cols], start=False, stop=False)
                last = pe.matmul(acc, lo[:, k, :], w_h[:, k, cols], start=False, stop=(k == KB - 1))
            return last

        def transposes(pe, src, dst=None):
            dst = ps_t if dst is None else dst
            for k in range(KB):
                last = pe.transpose(dst[:, k, :], src[:, k * P:(k + 1) * P], ident[:, :])
            return last

        def clusters(pe, acc, hi, lo):
            for k in range(KB):
                pe.matmul(acc, hi[:, k, :], cen[:, k, :], start=(k == 0), stop=False)
                last = pe.matmul(acc[:, 0:NCL], lo[:, k, :], cen[:, k, 0:NCL], start=False, stop=(k == KB - 1))
            return last

        def layer_norm_stats(dve, x, n, step, t, var_ready, norm_ready, sets=1, between=lambda: None):
            dve.bn_stats(bn[n][:, 0, :], x[:, 0:HALF])
            dve.bn_stats(bn[n][:, 1, :], x[:, HALF:EMB]).then_inc(step, 1)
            between()
            wait(dve, norm_ready, t + 1 - sets)
            wait_alone(dve, step, t + 1)
            dve.bn_aggr(moments[n][:, :], bn[n][:, :, :]).then_inc(var_ready, 1)

        def layer_norm_factors(pool, n, t, var_ready, step, norm_ready, used, saved, keep=None, sets=1):
            wait(pool, used, t + 1 - sets)
            if saved is not None:
                wait(pool, saved, t + 1 - sets)
            pool.wait_ge(var_ready, t + 1)
            pool.tensor_tensor(var_eps[n][:, :], moments[n][:, 1:2], eps[:, :], ALU.add).then_inc(step, 1)
            pool.tensor_tensor(minus_mean[n][:, :], moments[n][:, 0:1], minus_one[:, :], ALU.mult)
            pool.wait_ge(step, 2 * t + 1)
            pool.tensor_tensor(norm[n][:, 1:2], var_eps[n][:, :], minus_half[:, :], ALU.pow).then_inc(step, 1)
            pool.wait_ge(step, 2 * t + 2)
            pool.tensor_tensor(norm[n][:, 0:1], minus_mean[n][:, :], norm[n][:, 1:2], ALU.mult).then_inc(norm_ready, 1)
            if saved is not None:
                wait_alone(pool, norm_ready, t + 1)
                pool.tensor_copy(keep[:, ds(t, 1), :].rearrange("p a b -> p (a b)"),
                                 norm[n][:, :]).then_inc(saved, 1)

        def saved_norm(n, t):
            pair = norms[n][:, ds(t, 1), :].rearrange("p a b -> p (a b)")
            return pair[:, 0:1], pair[:, 1:2]

        def normed(act, y, x, minus_mean_rstd, rstd):
            return act.activation(y, x, ACT.Identity, bias=minus_mean_rstd, scale=rstd)

        def cluster_max(dve, acc, step, t, acc_read, ready):
            dve.tensor_reduce(logit_c[:, :], acc.rearrange("p (s c) -> p c s", s=2), axis=AX.X,
                              op=ALU.add).then_inc(acc_read, 1)
            dve.wait_ge(acc_read, t + 1)
            dve.tensor_reduce(neg_max[:, :], logit_c[:, :], axis=AX.X, op=ALU.max, negate=True).then_inc(step, 1)
            dve.wait_ge(step, 4 * t + 1)
            dve.tensor_scalar_mul(exp_bias[:, :], neg_max[:, :], INV_TEMPERATURE).then_inc(ready, 1)

        def cluster_exp(act):
            return act.activation(exp_c[:, :], logit_c[:, :], ACT.Exp, bias=exp_bias[:, :],
                                  scale=INV_TEMPERATURE, accum_out=exp_sum[:, :])

        def cluster_probs(dve, n, step, t):
            dve.reciprocal(exp_inv[:, :], exp_sum[:, :]).then_inc(step, 1)
            dve.wait_ge(step, 4 * t + 2)
            dve.tensor_scalar(prob_c[:, :], exp_c[:, :], exp_inv[:, :], None, ALU.mult).then_inc(step, 1)
            dve.wait_ge(step, 4 * t + 3)
            dve.reduce_max(prob_max[:, :], prob_c[:, :], AX.X).then_inc(step, 1)
            dve.tensor_tensor(best[n][:, :], best[n][:, :], prob_c[:, :], ALU.max).then_inc(best_set, 1)
            dve.wait_ge(step, 4 * t + 4)
            dve.tensor_scalar(token_on[n][:, ds(t, 1)], prob_max[:, :], THRESHOLD, None, ALU.is_gt)

        x_loaded, y1_ready, t1_done, hi1, lo1 = (sem("x_loaded"), sem("y1_ready"), sem("t1_done"), sem("hi1"),
                                                 sem("lo1"))
        const_set, ident_set, cen_loaded = sem("const_set"), sem("ident_set"), sem("cen_loaded")
        cen_t, cen_hi, cen_lo = sem("cen_t"), sem("cen_hi"), sem("cen_lo")
        assign_loaded, assign_set, onehot_set, bias_loaded = (sem("assign_loaded"), sem("assign_set"),
                                                              sem("onehot_set"), sem("bias_loaded"))
        w_loaded, wt_done, wt_hi, wt_lo = sem("w_loaded"), sem("wt_done"), sem("wt_hi"), sem("wt_lo")
        raw_loaded, q_step, q_summed, kv_moved = sem("raw_loaded"), sem("q_step"), sem("q_summed"), sem("kv_moved")
        proj_hi_set, proj_lo_set = sem("proj_hi_set"), sem("proj_lo_set")
        s_x_loaded = [sem(f"s_x_loaded{n}") for n in range(2)]
        s_step, s_var, s_power, s_norm = sem("s_step"), sem("s_var"), sem("s_power"), sem("s_norm")
        s_saved = sem("s_saved")
        s_y, s_t, s_hi, s_lo = sem("s_y"), sem("s_t"), sem("s_hi"), sem("s_lo")
        s_c, s_pair, s_fold = sem("s_c"), sem("s_pair"), sem("s_fold")
        s_cstep, s_cmax, s_cexp = sem("s_cstep"), sem("s_cmax"), sem("s_cexp")
        HD = HKV * D

        def scan(eng, step, prepare, group=lambda g, part: None, first_tile=lambda: None):
            def within(t):
                return 0 <= t < NT
            for i in (-2, -1, 0, 1):
                step(i, i % 2, within, i % GROUP, (i - 2) // 2, (i - 2) // GROUP)
            for part in range(3):
                prepare(0, part)

            def steps_of(m, first=False):
                for u in range(GROUP):
                    step(m * GROUP + (2 + u), u % 2, lambda t: True, (2 + u) % GROUP, m * 2 + u // 2, m)
                    if u < 3:
                        prepare(m + 1, u)
                    if u == 3:
                        group(m, 0)
                    elif u < 2 and not first:
                        group(m - 1, 1 + u)
            steps_of(0, True)
            with eng.Fori(1, KB - 1) as m:
                steps_of(m)
            for i in range(NT - 2, NT + 2):
                step(i, i % 2, within, i % GROUP, (i - 2) // 2, (i - 2) // GROUP)
                if i < NT:
                    group(NT // GROUP - 2, 1 + i % 2)
                if i == NT - 1:
                    first_tile()
                if i == NT:
                    prepare(KB, 0)
            for part in range(3):
                group(NT // GROUP - 1, part)

        def scan_slot(t):
            return x_ring[:, ds(t % 4, 1), :].rearrange("p a n -> p (a n)")

        with nc.Block() as block:
            @block.sync
            def _(sp):
                def step(i, par, ok):
                    if ok(i + 4):
                        t, n = i + 4, par
                        if not isinstance(t, int) or t >= 4:
                            wait_alone(sp, s_x_loaded[n], (t - n) * 8)
                            sp.wait_ge(s_y, t - 3)
                        sp.dma_start(scan_slot(t), x_d[ds(t, 1)].rearrange("a p n -> (a p) n")
                                     ).then_inc(s_x_loaded[n], 16)

                def weights(k, srcs):
                    if not isinstance(k, int) or k > 0:
                        wait_alone(sp, q_summed, k)
                        wait_alone(sp, kv_moved, k)
                    wait(sp, raw_loaded, 48 * k)
                    for src, a, b in zip(srcs, (0, EMB, EMB + HD), (EMB, EMB + HD, EMB + 2 * HD)):
                        sp.dma_start(proj_raw[:, a:b], src).then_inc(raw_loaded, 16)

                def block(k):
                    k = k + 1
                    wait_alone(sp, wt_done, k)
                    wait(sp, w_loaded, 16 * k)
                    sp.dma_start(w_raw, W[ds(k * P, P), :]).then_inc(w_loaded, 16)
                    weights(k, [w[ds(k * P, P)].rearrange("p d h -> p (d h)") for w in (Wq, Wk, Wv)])

                def within(t):
                    return 0 <= t < NT
                sp.dma_start(cen_raw, centroids).then_inc(cen_loaded, 16)
                sp.dma_start(assign_int, assignments.partition_broadcast(NCL)).then_inc(assign_loaded, 16)
                for t in range(3):
                    sp.dma_start(scan_slot(t), x_d[t]).then_inc(s_x_loaded[t % 2], 16)
                    if t == 1:
                        sp.wait_ge(s_x_loaded[0], 16)
                sp.dma_start(w_raw, W[0:P, :]).then_inc(w_loaded, 16)
                weights(0, [w[0:P].rearrange("p d h -> p (d h)") for w in (Wq, Wk, Wv)])
                sp.wait_ge(s_x_loaded[1], 16)
                sp.dma_start(scan_slot(3), x_d[3]).then_inc(s_x_loaded[1], 16)
                for i in (0, 1):
                    step(i, i % 2, within)
                block(0)
                with sp.Fori(0, KB - 2) as m:
                    for u in range(GROUP):
                        step(m * GROUP + (2 + u), u % 2, lambda t: True)
                        if u == 2:
                            block(m + 1)
                for i in (NT - 6, NT - 5):
                    step(i, i % 2, within)
                weights(KB, [b.rearrange("d h -> (d h)").partition_broadcast(P) for b in (bq, bk, bv)])
                for t in range(2):
                    wait_alone(sp, s_y, NT - 3 + t)
                    wait(sp, x_loaded, 16 * t)
                    sp.dma_start(slot(t), x_d[t]).then_inc(x_loaded, 16)
                sp.wait_ge(wt_done, KB)
                sp.dma_start(bias_raw, ffn_bias.partition_broadcast(P)).then_inc(bias_loaded, 16)

            @block.gpsimd
            def _(pool):
                pool.memset(ident[:, :], 0.0).then_inc(ident_set, 1)
                pool.memset(ones[:, :], 1.0)
                pool.memset(minus_half[:, :], -0.5)
                pool.memset(minus_one[:, :], -1.0)
                pool.memset(eps[:, :], EPS)
                pool.iota(cluster_int[:, :], pattern=[[0, 1]], base=0, channel_multiplier=1).then_inc(const_set, 1)
                pool.wait_ge(ident_set, 1)
                pool.affine_select(out=ident[:, :], in_=ident[:, :], compare_op=ALU.not_equal, fill=1.0, base=0,
                                   pattern=[[-1, P]], channel_multiplier=1).then_inc(ident_set, 1)
                pool.wait_ge(const_set, 1)

                def step(i, par, ok, q, p, g):
                    if ok(i + 2):
                        layer_norm_factors(pool, par, i + 2, s_var, s_power, s_norm, s_y, s_saved, norms[0], 2)

                def prepare(k, part):
                    if part == 0:
                        dst = proj_bias if is_int(k, KB) else proj_sum
                        total = dst[:, 0:HD].rearrange("p (g d) -> p g d", g=HKV)
                        heads = proj_raw[:, 0:EMB].rearrange("p (d g r) -> p g d r", g=HKV, r=SCALE)
                        pool.wait_ge(raw_loaded, 48 * k + 48)
                        wait(pool, proj_lo_set, k)
                        pool.tensor_tensor(total, heads[:, :, :, 0], heads[:, :, :, 1], ALU.add).then_inc(q_step, 1)
                        pool.wait_ge(q_step, 2 * k + 1)
                        pool.tensor_tensor(total, total, heads[:, :, :, 2], ALU.add).then_inc(q_step, 1)
                        pool.wait_ge(q_step, 2 * k + 2)
                        pool.tensor_tensor(total, total, heads[:, :, :, 3], ALU.add).then_inc(q_summed, 1)
                    if part == 2:
                        pool.wait_ge(proj_hi_set, k + 1)
                        pool.tensor_tensor(proj_lo[:, ds(k, 1), :].rearrange("p a n -> p (a n)"), proj_sum,
                                           proj_hi[:, ds(k, 1), :].rearrange("p a n -> p (a n)").bitcast(F32),
                                           ALU.subtract).then_inc(proj_lo_set, 1)
                scan(pool, step, prepare)

            @block.scalar
            def _(act):
                act.wait_ge(cen_t, 1)
                act.copy(cen[:, :, 0:NCL], ps_t[:, :, 0:NCL]).then_inc(cen_hi, 1)
                act.wait_ge(onehot_set, 1)

                def step(i, par, ok, q, p, g):
                    if ok(i):
                        act.wait_ge(s_t, i + 1)
                        wait(act, s_c, p)
                        act.copy(scan_hi[q // 2][:, :, par, :], scan_ps[par]).then_inc(s_hi, 1)
                    if ok(i + 1):
                        t, n = i + 1, (par + 1) % 2
                        act.wait_ge(s_norm, t + 1)
                        wait(act, s_t, t - 1)
                        normed(act, y_tok[n], scan_slot(t), norm[n][:, 0:1], norm[n][:, 1:2]).then_inc(s_y, 1)
                    if par == 0 and ok(i - 2):
                        act.wait_ge(s_c, p + 1)
                        wait(act, s_fold, p)
                        act.copy(pair_sums, pair_ps).then_inc(s_pair, 1)

                def group(g, part):
                    if part == 1:
                        act.wait_ge(s_cmax, g + 1)
                        act.activation(group_exp, group_exp_in, ACT.Exp, scale=INV_TEMPERATURE).then_inc(s_cexp, 1)

                def move_kv(k, dst):
                    act.wait_ge(raw_loaded, 48 * k + 48)
                    for a, b in ((EMB, HD), (EMB + HD, 2 * HD)):
                        moved = act.copy(dst[:, b:b + HD].rearrange("p (g d) -> p d g", g=HKV),
                                         proj_raw[:, a:a + HD].rearrange("p (d g) -> p d g", g=HKV))
                    moved.then_inc(kv_moved, 1)

                def prepare(k, part):
                    if part == 0:
                        wait(act, proj_lo_set, k)
                        move_kv(k, proj_bias if is_int(k, KB) else proj_sum)
                    if part == 1:
                        act.wait_ge(q_summed, k + 1)
                        act.wait_ge(kv_moved, k + 1)
                        act.copy(proj_hi[:, ds(k, 1), :].rearrange("p a n -> p (a n)"),
                                 proj_sum).then_inc(proj_hi_set, 1)
                    if part == 2:
                        act.wait_ge(wt_done, k + 1)
                        act.copy(w_hi[:, :, ds(k * P, P)], weight_ps).then_inc(wt_hi, 1)

                def first_tile():
                    act.wait_ge(x_loaded, 16)
                    act.wait_ge(s_t, NT - 1)
                    normed(act, y_tok[0], slot(0), *saved_norm(0, 0)).then_inc(y1_ready, 1)
                    act.wait_ge(t1_done, 1)
                    act.wait_ge(s_c, NT // 2 - 1)
                    act.copy(y_hi[0][:, :, :], ps_t[:, :, :]).then_inc(hi1, 1)
                scan(act, step, prepare, group, first_tile)

            @block.vector
            def _(dve):
                dve.memset(best[0][:, :], 0.0)
                dve.memset(best[1][:, :], 0.0)
                dve.wait_ge(ident_set, 2)
                dve.reduce_sum(own_t[:, :], ident[:, :].rearrange("p (c t) -> p t c", t=T4), AX.X)
                dve.wait_ge(const_set, 1)
                dve.tensor_copy(cluster_id[:, :], cluster_int[:, :])
                dve.wait_ge(assign_loaded, 16)
                dve.tensor_copy(assign, assign_int).then_inc(assign_set, 1)
                dve.wait_ge(assign_set, 1)
                dve.tensor_scalar(onehot[:, :], assign, cluster_id[:, :], None, ALU.is_equal).then_inc(onehot_set, 1)
                dve.reduce_sum(fold, ident[:, :].rearrange("p (s c) -> p c s", s=2), AX.X)
                dve.wait_ge(cen_hi, 1)
                dve.tensor_tensor(cen[:, :, NCL:2 * NCL], ps_t[:, :, 0:NCL], cen[:, :, 0:NCL].bitcast(F32),
                                  ALU.subtract).then_inc(cen_lo, 1)

                def step(i, par, ok, q, p, g):
                    def low_part():
                        if ok(i):
                            dve.wait_ge(s_hi, i + 1)
                            dve.tensor_tensor(scan_lo[q // 2][:, :, par, :], scan_ps[par],
                                              scan_hi[q // 2][:, :, par, :].bitcast(F32),
                                              ALU.subtract).then_inc(s_lo, 1)
                    if ok(i + 2):
                        t = i + 2
                        dve.wait_ge(s_x_loaded[par], (t - par) * 8 + 16)
                        layer_norm_stats(dve, scan_slot(t), par, s_step, t, s_var, s_norm, 2, low_part)
                    else:
                        low_part()

                def group(g, part):
                    by_tile = "p (t c) -> p t c"
                    wide = [P, GROUP, NCL]
                    if part == 0:
                        dve.wait_ge(s_fold, g * 2 + 2)
                        logits = group_ps.rearrange(by_tile, c=NCL)
                        dve.tensor_reduce(group_max, logits, axis=AX.X, op=ALU.max).then_inc(s_cstep, 1)
                        dve.wait_ge(s_cstep, g * 6 + 1)
                        dve.tensor_tensor(group_exp_in.rearrange(by_tile, c=NCL), logits,
                                          group_max.unsqueeze(2).to_broadcast(wide), ALU.subtract).then_inc(s_cmax, 1)
                    if part == 2:
                        dve.wait_ge(s_cexp, g + 1)
                        dve.reduce_sum(group_sum, group_exp.rearrange(by_tile, c=NCL), AX.X).then_inc(s_cstep, 1)
                        dve.wait_ge(s_cstep, g * 6 + 2)
                        dve.reciprocal(group_inv, group_sum).then_inc(s_cstep, 1)
                        dve.wait_ge(s_cstep, g * 6 + 3)
                        dve.tensor_tensor(group_exp.rearrange(by_tile, c=NCL), group_exp.rearrange(by_tile, c=NCL),
                                          group_inv.unsqueeze(2).to_broadcast(wide), ALU.mult).then_inc(s_cstep, 1)
                        dve.wait_ge(s_cstep, g * 6 + 4)
                        dve.reduce_max(group_top, group_exp.rearrange(by_tile, c=NCL), AX.X).then_inc(s_cstep, 1)
                        dve.reduce_max(group_best, group_exp.rearrange("p (t c) -> p c t", c=NCL),
                                       AX.X).then_inc(s_cstep, 1)
                        dve.wait_ge(s_cstep, g * 6 + 5)
                        dve.tensor_scalar(token_on[0][:, ds(g * GROUP, GROUP)], group_top, THRESHOLD, None, ALU.is_gt)
                        dve.wait_ge(s_cstep, g * 6 + 6)
                        dve.tensor_tensor(best[0][:, :], best[0][:, :], group_best, ALU.max)

                def prepare(k, part):
                    if part == 2:
                        dve.wait_ge(wt_hi, k + 1)
                        dve.tensor_tensor(w_lo[:, :, ds(k * P, P)], weight_ps,
                                          w_hi[:, :, ds(k * P, P)].bitcast(F32), ALU.subtract).then_inc(wt_lo, 1)

                def first_tile():
                    dve.wait_ge(hi1, 1)
                    dve.tensor_tensor(y_lo[0][:, :, :], ps_t[:, :, :], y_hi[0][:, :, :].bitcast(F32),
                                      ALU.subtract).then_inc(lo1, 1)
                scan(dve, step, prepare, group, first_tile)

            @block.tensor
            def _(pe):
                pe.wait_ge(ident_set, 2)
                pe.wait_ge(cen_loaded, 16)
                for k in range(KB):
                    last = pe.transpose(ps_t[:, k, 0:NCL], cen_raw[:, k * P:(k + 1) * P], ident[0:NCL, 0:NCL])
                last.then_inc(cen_t, 1)
                pe.wait_ge(cen_lo, 1)

                def step(i, par, ok, q, p, g):
                    if ok(i):
                        pe.wait_ge(s_y, i + 1)
                        wait(pe, s_lo, i - 1)
                        transposes(pe, y_tok[par], scan_ps[par]).then_inc(s_t, 1)
                    if par == 0 and ok(i - 2):
                        hi, lo = scan_hi[1 - q // 2], scan_lo[1 - q // 2]

                        def low(k):
                            pe.matmul(pair_ps[0:NCL, :], cen[:, k, 0:NCL], lo[:, k, :, :], start=False, stop=False)
                        pe.wait_ge(s_lo, i)
                        wait(pe, s_pair, p)
                        for k in range(KB):
                            if k == KB - 1:
                                low(k)
                            last = pe.matmul(pair_ps, cen[:, k, :], hi[:, k, :, :], start=(k == 0),
                                             stop=(k == KB - 1))
                            if k < KB - 1:
                                low(k)
                        last.then_inc(s_c, 1)
                    if par == 1 and ok(i - 3):
                        pe.wait_ge(s_pair, p + 1)
                        if q == 3:
                            wait(pe, s_cmax, g)
                        for n in range(2):
                            at = ((q + 1) % GROUP + n) * NCL
                            last = pe.matmul(group_ps[:, at:at + NCL], pair_sums[:, n * P:(n + 1) * P], fold,
                                             start=True, stop=True)
                        last.then_inc(s_fold, 1)

                def prepare(k, part):
                    if part == 1:
                        pe.wait_ge(w_loaded, 16 * k + 16)
                        wait(pe, wt_lo, k)
                        transposes(pe, w_raw, weight_ps).then_inc(wt_done, 1)

                def first_tile():
                    pe.wait_ge(y1_ready, 1)
                    pe.wait_ge(s_lo, NT - 1)
                    transposes(pe, y_tok[0]).then_inc(t1_done, 1)
                scan(pe, step, prepare, first_tile=first_tile)

        scan_memory.close()
        work2 = sb("work2", [P, 5120])
        q_diag = work2[:, 0:1024]
        k_diag = work2[:, 1024:2048]
        mask_half = work2[:, 2048:3072]
        bias_half = work2[:, 3072:4096]
        qkv_tok = work2[:, 4096:4864]
        v_head = work2[:, 4864:5120]
        cluster_on = mask_half[0:NCL, 0:P // 2].bitcast(BF16)

        m_hit, m_count, m_on = sem("m_hit"), sem("m_count"), sem("m_on")
        m_rows, m_mask, m_bias = sem("m_rows"), sem("m_mask"), sem("m_bias")

        def select_vector(dve, n, acc):
            if n == 1:
                dve.wait_ge(best_set, NT)
            dve.tensor_scalar(hit[:, :], best[n][:, :], THRESHOLD, None, ALU.is_gt).then_inc(m_hit, 1)
            dve.wait_ge(m_count, n + 1)
            dve.tensor_scalar(cluster_on, acc[0:NCL, 0:P], 1.0, 0.5, ALU.min, ALU.mult).then_inc(m_on, 1)

        def select_bias(dve, n):
            dve.wait_ge(bias_loaded, 16 * n + 16)
            dve.wait_ge(m_mask, n + 1)
            dve.tensor_tensor(bias_half, bias_raw, mask_half, ALU.mult).then_inc(m_bias, 1)
            dve.wait_ge(m_bias, n + 1)

        def select_tensor(pe, n, acc):
            pe.wait_ge(m_hit, n + 1)
            pe.matmul(acc[0:NCL, 0:P], hit[:, :], ones[:, :], start=True, stop=True).then_inc(m_count, 1)
            pe.wait_ge(m_on, n + 1)
            for h in range(2):
                last = pe.matmul(acc[:, h * HALF:(h + 1) * HALF], cluster_on,
                                 onehot[:, h * HALF:(h + 1) * HALF], start=True, stop=True)
            last.then_inc(m_rows, 1)

        def select_scalar(act, n, acc):
            act.wait_ge(m_rows, n + 1)
            act.copy(mask_half, acc[:, :]).then_inc(m_mask, 1)

        x2_ready, x2_stored = sem("x2_ready"), sem("x2_stored")
        y2_ready, y3_ready = sem("y2_ready"), sem("y3_ready")
        t2_done, t3_done = sem("t2_done"), sem("t3_done")
        hi2, hi3, lo2, lo3 = sem("hi2"), sem("hi3"), sem("lo2"), sem("lo3")
        ffn_done, ffn_read, x1_step = sem("ffn_done"), sem("ffn_read"), sem("x1_step")
        ln2_step, var2, power2, norm2 = sem("ln2_step"), sem("var2"), sem("power2"), sem("norm2")
        saved3, zeroed = sem("saved3"), sem("zeroed")
        ln3_step, var3, power3, norm3 = sem("ln3_step"), sem("var3"), sem("power3"), sem("norm3")
        proj_done, proj_read, qk_stored, v_stored = (sem("proj_done"), sem("proj_read"), sem("qk_stored"),
                                                     sem("v_stored"))
        q_loaded, k_loaded, v_loaded = sem("q_loaded"), sem("k_loaded"), sem("v_loaded")
        q_diag_ready, v_diag_ready = sem("q_diag_ready"), sem("v_diag_ready")
        scores_done, scores_read, exp_ready = sem("scores_done"), sem("scores_read"), sem("exp_ready")
        soft_step, probs_ready, heads_done = sem("soft_step"), sem("probs_ready"), sem("heads_done")
        o_ready, o_stored, o_loaded = sem("o_ready"), sem("o_stored"), sem("o_loaded")
        c_done, c_step, c_read, c_max, c_exp = sem("c_done"), sem("c_step"), sem("c_read"), sem("c_max"), sem("c_exp")

        EARLY = 2
        f_x_loaded = [sem(f"f_x_loaded{n}") for n in range(2)]
        f_y, f_t, f_hi, f_lo = sem("f_y"), sem("f_t"), sem("f_hi"), sem("f_lo")
        f_ffn, f_read, f_step, f_out = sem("f_ffn"), sem("f_read"), sem("f_step"), sem("f_out")

        def f_slot(t):
            return slot(t + 2)

        def f_acc(t, par):
            if isinstance(t, int) and t < EARLY:
                return (ps_b, ps_s)[t]
            return (ps_a, ps_b)[par]

        def finish(eng, emit):
            def ok(t):
                return 0 <= t < NT

            def todo(t):
                return EARLY <= t < NT
            for i in range(-2, 4):
                emit(i, i % 2, ok, todo)
            with eng.Fori(2, (NT - 2) // 2) as m:
                for u in range(2):
                    emit(m * 2 + u, u, lambda t: True, lambda t: True)
            for i in (NT - 2, NT - 1):
                emit(i, i % 2, ok, todo)

        def main(eng, emit):
            for i in range(-1, 4):
                emit(i, lambda t: 0 <= t < NT)
            with eng.Fori(4, NT - 2) as i:
                emit(i, lambda t: True)
            for i in range(NT - 2, NT + 3):
                emit(i, lambda t: 0 <= t < NT)

        def prob_block(r, j):
            return (j * R4 + r) * D

        with nc.Block() as block:
            @block.sync
            def _(sp):
                def load(t):
                    wait(sp, x_loaded, 16 * t)
                    sp.dma_start(slot(t), x_d[ds(t, 1)].rearrange("a p n -> (a p) n")).then_inc(x_loaded, 16)

                def store(t, a, b, stored):
                    sp.dma_start(qkv_d[ds(t, 1), a:b].rearrange("a s k e -> (a k) s e"),
                                 qkv_tok[:, a * D:b * D].rearrange("p (s e) -> p s e", e=D)).then_inc(stored, 16)

                def step(i, ok):
                    if ok(i - 3):
                        t = i - 3
                        sp.wait_ge(x2_ready, t + 1)
                        sp.dma_start(x2_d[ds(t, 1)].rearrange("a p n -> (a p) n"), slot(t)).then_inc(x2_stored, 16)
                    if ok(i + 2) and not is_int(i, -1):
                        if ok(i - 3):
                            sp.wait_ge(x2_stored, 16 * (i - 2))
                            sp.wait_ge(y3_ready, i - 2)
                        load(i + 2)
                    if is_int(i, NT):
                        sp.wait_ge(x2_stored, 16 * (NT - 3))
                        sp.wait_ge(y3_ready, NT - 3)
                        for t in range(EARLY):
                            sp.dma_start(f_slot(t), x2_d[t]).then_inc(f_x_loaded[t], 16)
                    if is_int(i, NT + 1):
                        sp.wait_ge(x2_stored, 16 * (NT - 2))
                        sp.wait_ge(y3_ready, NT - 2)
                        sp.wait_ge(f_x_loaded[0], 16)
                        sp.dma_start(f_slot(EARLY), x2_d[EARLY]).then_inc(f_x_loaded[0], 16)
                    if ok(i - 1):
                        t = i - 1
                        sp.wait_ge(proj_read, 2 * t + 1)
                        store(t, 0, 2 * HKV, qk_stored)
                        sp.wait_ge(qk_stored, 16 * t + 16)
                        q, k = (qkv_d[ds(t, 1), HKV * s:HKV * (s + 1)] for s in range(2))
                        by_row_block = "a g (t r j) e -> r (a g t) (j e)"
                        wait(sp, q_diag_ready, t)
                        sp.dma_start(q_head[:, :], q.rearrange(by_row_block, t=T4, r=R4)).then_inc(q_loaded, 16)
                        wait(sp, scores_done, t)
                        for r in range(R4):
                            sp.dma_start(k_diag[32 * r:32 * r + 32, r * J8 * D:(r + 1) * J8 * D],
                                         k.rearrange(by_row_block, t=T4, r=R4)[r]).then_inc(k_loaded, 16)
                        sp.wait_ge(proj_read, 2 * t + 2)
                        store(t, 2 * HKV, 3 * HKV, v_stored)
                    if ok(i - 2):
                        t = i - 2
                        sp.wait_ge(o_stored, 16 * t + 16)
                        wait(sp, x2_ready, t)
                        sp.dma_start(o_tok[:, :].rearrange("p (g d) -> p g d", g=HKV),
                                     o_d[ds(t, 1)].rearrange("a g k d -> (a k) g d")).then_inc(o_loaded, 16)
                    if ok(i - 1):
                        t = i - 1
                        sp.wait_ge(v_stored, 16 * t + 16)
                        v = qkv_d[ds(t, 1), 2 * HKV:3 * HKV]
                        wait(sp, v_diag_ready, t)
                        sp.dma_start(v_head, v.rearrange("a g (n j) e -> (a n) g (j e)", j=J8)).then_inc(v_loaded, 16)
                sp.wait_ge(zeroed, 1)
                main(sp, step)
                sp.wait_ge(probs_ready, NT)
                sp.dma_start(bias_raw, ffn_bias.partition_broadcast(P)).then_inc(bias_loaded, 16)

                sp.wait_ge(x2_stored, 16 * NT)
                sp.wait_ge(y3_ready, NT)

                def finish_load(t, n):
                    wait(sp, f_x_loaded[n], (t - n) * 8)
                    sp.dma_start(f_slot(t), x2_d[ds(t, 1)].rearrange("a p n -> (a p) n")).then_inc(f_x_loaded[n], 16)

                def finish_step(i, par, ok):
                    if ok(i):
                        wait_alone(sp, f_step, 3 * i + 3)
                        wait(sp, f_out, 16 * i)
                        sp.dma_start(out_d[ds(i, 1)].rearrange("a p n -> (a p) n"), f_slot(i)).then_inc(f_out, 16)
                    if ok(i + 4) and not is_int(i, EARLY - 4):
                        if ok(i - 1):
                            sp.wait_ge(f_out, 16 * i)
                        finish_load(i + 4, par)
                for i in (-2, -1):
                    finish_step(i, i % 2, lambda t: 0 <= t < NT)
                finish_step(0, 0, lambda t: 0 <= t < NT)
                finish_step(1, 1, lambda t: 0 <= t < NT)
                with sp.Fori(1, (NT - 4) // 2) as m:
                    for u in range(2):
                        finish_step(m * 2 + u, u, lambda t: True)
                for i in range(NT - 4, NT):
                    finish_step(i, i % 2, lambda t: 0 <= t < NT)
                sp.wait_ge(f_out, 16 * NT)

            @block.gpsimd
            def _(pool):
                def step(i, ok):
                    if ok(i - 3):
                        layer_norm_factors(pool, 1, i - 3, var3, power3, norm3, y3_ready, saved3,
                                           norms[1])
                    if ok(i):
                        layer_norm_factors(pool, 0, i, var2, power2, norm2, y2_ready, None)
                pool.memset(v_diag, 0.0)
                pool.memset(k_diag, 0.0).then_inc(zeroed, 1)
                main(pool, step)

            @block.scalar
            def _(act):
                def early_norm(t):
                    act.wait_ge(f_x_loaded[t % 2], 16 * (t // 2) + 16)
                    if t == 0:
                        act.wait_ge(t2_done, NT)
                    else:
                        act.wait_ge(f_t, t)
                    normed(act, y_tok[0], f_slot(t), *saved_norm(1, t)).then_inc(f_y, 1)

                def early_high(t):
                    act.wait_ge(f_t, t + 1)
                    act.copy(y_hi[1][:, :, :], ps_t[:, :, :]).then_inc(f_hi, 1)

                def step(i, ok):
                    if ok(i + 1) and not is_int(i, -1):
                        t = i + 1
                        act.wait_ge(x_loaded, 16 * t + 16)
                        wait(act, t2_done, i)
                        normed(act, y_tok[0], slot(t), *saved_norm(0, t)).then_inc(y1_ready, 1)
                    if ok(i - 2):
                        t = i - 2
                        act.wait_ge(q_loaded, 16 * t + 16)
                        wait(act, scores_done, t)
                        for b in range(T4):
                            last = act.activation(q_diag.rearrange("p (j t d) -> p j t d", t=T4, d=D)[:, :, b, :],
                                                  q_head[:, :].rearrange("p (j d) -> p j d", d=D), ACT.Identity,
                                                  scale=own_t[:, b:b + 1])
                        last.then_inc(q_diag_ready, 1)
                    if is_int(i, NT + 1):
                        early_norm(1)
                    if ok(i - 3):
                        t = i - 3
                        act.wait_ge(norm3, t + 1)
                        wait(act, t3_done, t)
                        normed(act, y_tok[1], slot(t), norm[1][:, 0:1], norm[1][:, 1:2]).then_inc(y3_ready, 1)
                        act.wait_ge(t3_done, t + 1)
                        act.copy(y_hi[0][:, :, :], ps_t[:, :, :]).then_inc(hi3, 1)
                    if ok(i - 2):
                        act.wait_ge(scores_read, i - 1)
                        act.activation(probs, probs, ACT.Exp, scale=1.0 / float(np.sqrt(D))).then_inc(exp_ready, 1)
                    if ok(i + 1) and not is_int(i, -1):
                        act.wait_ge(t1_done, i + 2)
                        act.copy(y_hi[0][:, :, :], ps_t[:, :, :]).then_inc(hi1, 1)
                    if is_int(i, -1):
                        select_scalar(act, 0, ps_s)
                    if ok(i):
                        act.wait_ge(norm2, i + 1)
                        act.wait_ge(t1_done, i + 2 if ok(i + 1) else NT)
                        normed(act, y_tok[0], slot(i), norm[0][:, 0:1], norm[0][:, 1:2]).then_inc(y2_ready, 1)
                    if is_int(i, NT):
                        early_norm(0)
                    if is_int(i, NT + 1):
                        act.wait_ge(f_ffn, 2)
                        early_high(1)
                        early_norm(2)
                    if ok(i - 3):
                        act.wait_ge(c_max, i - 2)
                        cluster_exp(act).then_inc(c_exp, 1)
                    if ok(i - 2):
                        act.wait_ge(heads_done, i - 1)
                        wait(act, o_stored, 16 * (i - 2))
                        act.copy(o_head[:, :], ps_s[:, 0:HKV * D]).then_inc(o_ready, 1)
                        act.wait_ge(o_ready, i - 1)
                        act.dma_start(o_d[ds(i - 2, 1)].rearrange("a g (t r j) d -> r (a g t) (j d)", t=T4, r=R4),
                                      o_head[:, :]).then_inc(o_stored, 16)
                    if ok(i):
                        act.wait_ge(t2_done, i + 1)
                        act.copy(y_hi[1][:, :, :], ps_t[:, :, :]).then_inc(hi2, 1)
                    if is_int(i, NT):
                        early_high(0)
                main(act, step)

                act.wait_ge(saved3, NT)
                def finish_step(i, par, ok, todo):
                    if todo(i + 1):
                        n = (par + 1) % 2
                        act.wait_ge(f_t, i + 2)
                        act.copy(y_hi[n][:, :, :], ps_t[:, :, :]).then_inc(f_hi, 1)
                    if todo(i + 2) and not is_int(i, EARLY - 2):
                        t = i + 2
                        act.wait_ge(f_x_loaded[par], (t - par) * 8 + 16)
                        wait(act, f_t, i + 1)
                        normed(act, y_tok[par], f_slot(t), *saved_norm(1, t)).then_inc(f_y, 1)
                    if is_int(i, EARLY - 1):
                        select_scalar(act, 1, ps_t_flat)
                finish(act, finish_step)

            @block.vector
            def _(dve):
                def low_part(n, hi_sem, lo_sem, t):
                    dve.wait_ge(hi_sem, t + 1)
                    dve.tensor_tensor(y_lo[n][:, :, :], ps_t[:, :, :], y_hi[n][:, :, :].bitcast(F32),
                                      ALU.subtract).then_inc(lo_sem, 1)

                def ffn_half(i, n):
                    h = 1 - n
                    cols = slice(h * HALF, (h + 1) * HALF)
                    dve.wait_ge(ffn_done, 2 * i + n + 1)
                    dve.scalar_tensor_tensor(ffn_part[:, n, :], ps_a[:, cols], token_on[0][:, ds(i, 1)],
                                             mask_half[:, cols], ALU.mult, ALU.mult).then_inc(ffn_read, 1)
                    dve.wait_ge(ffn_read, 2 * i + n + 1)
                    dve.tensor_tensor(slot(i)[:, cols], slot(i)[:, cols], ffn_part[:, n, :],
                                      ALU.add).then_inc(x1_step, 1)

                def add_bias(t, n, cols, stored):
                    wait(dve, stored, 16 * t)
                    dve.wait_ge(proj_done, 2 * t + n + 1)
                    dve.tensor_tensor(qkv_tok[:, cols], ps_b[:, cols], proj_bias[:, cols],
                                      ALU.add).then_inc(proj_read, 1)

                def step(i, ok):
                    if ok(i):
                        dve.wait_ge(x_loaded, 16 * i + 16)
                        dve.wait_ge(y1_ready, i + 1)
                        dve.scalar_tensor_tensor(slot(i), bias_half, token_on[0][:, ds(i, 1)], slot(i), ALU.mult,
                                                 ALU.add).then_inc(x1_step, 1)
                    if ok(i):
                        dve.wait_ge(x1_step, 3 * i + 1)
                        ffn_half(i, 0)
                    if ok(i - 3):
                        t = i - 3
                        dve.wait_ge(o_loaded, 16 * t + 16)
                        dve.wait_ge(y2_ready, t + 1)
                        x2 = slot(t)
                        x2_v = x2.rearrange("p (d g r) -> p d g r", g=HKV, r=SCALE)
                        o_v = o_tok[:, :].rearrange("p (g d) -> p d g", g=HKV)
                        o_v = o_v.unsqueeze(3).to_broadcast([P, D, HKV, SCALE])
                        dve.tensor_tensor(x2_v, x2_v, o_v, ALU.add).then_inc(x2_ready, 1)
                        wait_alone(dve, x2_ready, t + 1)
                        layer_norm_stats(dve, x2, 1, ln3_step, t, var3, norm3)
                    if ok(i - 2):
                        t = i - 2
                        dve.wait_ge(v_loaded, 16 * t + 16)
                        wait(dve, heads_done, t)
                        for b in range(T4):
                            last = dve.transpose(v_diag[32 * b:32 * b + 32, b:EMB:T4], v_head[32 * b:32 * b + 32, :])
                        last.then_inc(v_diag_ready, 1)
                    if ok(i):
                        ffn_half(i, 1)
                    if ok(i - 2):
                        t = i - 2
                        groups = "p (c e) -> p c e"
                        wide = [P, HEADS, D]
                        probs_v = probs.rearrange(groups, e=D)
                        scores_v = ps_s[:, :].rearrange(groups, e=D)
                        dve.wait_ge(scores_done, t + 1)
                        dve.reduce_max(row_max[:, :], scores_v, AX.X).then_inc(soft_step, 1)
                        dve.wait_ge(soft_step, 4 * t + 1)
                        dve.tensor_tensor(probs_v, scores_v, row_max[:, :].unsqueeze(2).to_broadcast(wide),
                                          ALU.subtract).then_inc(scores_read, 1)
                    if ok(i - 3):
                        low_part(0, hi3, lo3, i - 3)
                    if ok(i - 2):
                        dve.wait_ge(exp_ready, t + 1)
                        dve.reduce_sum(row_sum[:, :], probs_v, AX.X).then_inc(soft_step, 1)
                    if is_int(i, 0):
                        low_part(0, hi1, lo1, 1)
                    if ok(i):
                        wait_alone(dve, x1_step, 3 * i + 3)
                        layer_norm_stats(dve, slot(i), 0, ln2_step, i, var2, norm2)
                    if ok(i - 1):
                        add_bias(i - 1, 0, slice(0, HALF), qk_stored)
                    if ok(i - 2):
                        dve.wait_ge(soft_step, 4 * t + 2)
                        dve.reciprocal(row_inv[:, :], row_sum[:, :]).then_inc(soft_step, 1)
                        dve.wait_ge(soft_step, 4 * t + 3)
                        dve.tensor_tensor(probs_v, probs_v, row_inv[:, :].unsqueeze(2).to_broadcast(wide),
                                          ALU.mult).then_inc(soft_step, 1)
                        dve.wait_ge(soft_step, 4 * t + 4)
                        wait(dve, heads_done, t)
                        dve.transpose(probs_t, probs).then_inc(probs_ready, 1)
                    if ok(i + 1) and not is_int(i, -1) and not is_int(i, 0):
                        low_part(0, hi1, lo1, i + 1)
                    if is_int(i, -1):
                        select_bias(dve, 0)
                    if ok(i - 3):
                        dve.wait_ge(c_done, i - 2)
                        cluster_max(dve, ps_a[:, 0:2 * NCL], c_step, i - 3, c_read, c_max)
                    if ok(i - 1):
                        add_bias(i - 1, 1, slice(HALF, PROJ), v_stored)
                    if ok(i - 3):
                        dve.wait_ge(c_exp, i - 2)
                        cluster_probs(dve, 1, c_step, i - 3)
                    if ok(i):
                        low_part(1, hi2, lo2, i)
                    for t in range(EARLY):
                        if is_int(i, NT + t):
                            low_part(1, f_hi, f_lo, t)
                select_vector(dve, 0, ps_s)
                dve.wait_ge(zeroed, 1)
                main(dve, step)

                def finish_low(t, n):
                    dve.wait_ge(f_hi, t + 1)
                    dve.tensor_tensor(y_lo[n][:, :, :], ps_t[:, :, :], y_hi[n][:, :, :].bitcast(F32),
                                      ALU.subtract).then_inc(f_lo, 1)

                def finish_step(i, par, ok, todo):
                    if todo(i + 1) and not is_int(i, EARLY - 1):
                        finish_low(i + 1, (par + 1) % 2)
                    if ok(i):
                        dve.wait_ge(f_y, i + 1)
                        acc = f_acc(i, par)
                        on = token_on[1][:, ds(i, 1)]
                        dve.scalar_tensor_tensor(f_slot(i), bias_half, on, f_slot(i), ALU.mult, ALU.add).then_inc(f_step, 1)
                        dve.wait_ge(f_step, 3 * i + 1)
                        for h in range(2):
                            cols = slice(h * HALF, (h + 1) * HALF)
                            dve.wait_ge(f_ffn, 2 * i + h + 1)
                            dve.scalar_tensor_tensor(ffn_part[:, h, :], acc[:, cols], on, mask_half[:, cols],
                                                     ALU.mult, ALU.mult).then_inc(f_read, 1)
                            dve.wait_ge(f_read, 2 * i + h + 1)
                            dve.tensor_tensor(f_slot(i)[:, cols], f_slot(i)[:, cols], ffn_part[:, h, :],
                                              ALU.add).then_inc(f_step, 1)
                finish_low(EARLY, EARLY % 2)
                select_vector(dve, 1, ps_t_flat)
                select_bias(dve, 1)
                finish(dve, finish_step)

            @block.tensor
            def _(pe):
                def projection(t, cols, amid=lambda: None):
                    pe.wait_ge(lo2, t + 1)
                    wait(pe, proj_read, 2 * t)
                    product(pe, ps_b[:, cols], y_hi[1], y_lo[1], proj_hi, proj_lo, cols,
                            amid).then_inc(proj_done, 1)

                def cluster_transposes(i, ok):
                    pe.wait_ge(y3_ready, i - 2)
                    pe.wait_ge(lo2, i if ok(i) else NT)
                    transposes(pe, y_tok[1]).then_inc(t3_done, 1)

                def projection_transposes(i, ok):
                    pe.wait_ge(y2_ready, i + 1)
                    if ok(i + 1):
                        pe.wait_ge(lo1, i + 2)
                    else:
                        pe.wait_ge(lo3, i - 2)
                    transposes(pe, y_tok[0]).then_inc(t2_done, 1)

                def early_transposes(t):
                    pe.wait_ge(f_y, t + 1)
                    pe.wait_ge(lo3, NT - 2 + t)
                    transposes(pe, y_tok[0]).then_inc(f_t, 1)

                def early_ffn(t, h):
                    cols = slice(h * HALF, (h + 1) * HALF)
                    pe.wait_ge(f_lo, t + 1)
                    if t == 0:
                        pe.wait_ge(proj_read, 2 * NT)
                    else:
                        pe.wait_ge(o_ready, NT)
                    product(pe, f_acc(t, t)[:, cols], y_hi[1], y_lo[1], w_hi, w_lo, cols).then_inc(f_ffn, 1)

                def step(i, ok):
                    if is_int(i, NT + 2):
                        early_ffn(1, 0)
                        early_ffn(1, 1)
                    if ok(i):
                        pe.wait_ge(lo1, i + 1)
                        wait(pe, ffn_read, 2 * i)
                        product(pe, ps_a[:, HALF:EMB], y_hi[0], y_lo[0], w_hi, w_lo,
                                slice(HALF, EMB)).then_inc(ffn_done, 1)
                        if is_int(i, 1):
                            projection_transposes(0, ok)
                        if ok(i - 4):
                            pe.wait_ge(c_read, i - 3)
                        product(pe, ps_a[:, 0:HALF], y_hi[0], y_lo[0], w_hi, w_lo,
                                slice(0, HALF)).then_inc(ffn_done, 1)
                    if ok(i - 2):
                        t = i - 2
                        pe.wait_ge(q_diag_ready, t + 1)
                        pe.wait_ge(k_loaded, 16 * R4 * (t + 1))
                        wait(pe, o_ready, t)
                        k_blocks = k_diag.rearrange("p (r j e) -> p j r e", r=R4, e=D)
                        for j in range(J8):
                            last = pe.matmul(ps_s[:, j * P:(j + 1) * P], q_diag[:, j * P:(j + 1) * P],
                                             k_blocks[:, j, :, :], start=True, stop=True)
                        last.then_inc(scores_done, 1)
                    if is_int(i, NT + 1):
                        early_ffn(0, 0)
                    if ok(i - 3) and not ok(i - 1):
                        cluster_transposes(i, ok)
                    if is_int(i, NT + 1):
                        early_ffn(0, 1)
                        early_transposes(1)
                    if ok(i - 1):
                        if ok(i - 3) and not is_int(i, NT):
                            projection(i - 1, slice(0, HALF), lambda: cluster_transposes(i, ok))
                        else:
                            projection(i - 1, slice(0, HALF))
                            if ok(i - 3):
                                cluster_transposes(i, ok)
                    if ok(i - 3):
                        pe.wait_ge(lo3, i - 2)
                        pe.wait_ge(ffn_read, 2 * i + 2 if ok(i) else 2 * NT)
                        clusters(pe, ps_a[:, 0:2 * NCL], y_hi[0], y_lo[0]).then_inc(c_done, 1)
                    if ok(i + 1) and not is_int(i, -1):
                        pe.wait_ge(y1_ready, i + 2)
                        if ok(i - 3):
                            pe.wait_ge(lo3, i - 2)
                        else:
                            wait(pe, lo2, i)
                        transposes(pe, y_tok[0]).then_inc(t1_done, 1)
                    if is_int(i, -1):
                        select_tensor(pe, 0, ps_s)
                    if ok(i - 1):
                        projection(i - 1, slice(HALF, PROJ))
                    if ok(i - 2):
                        t = i - 2
                        pe.wait_ge(probs_ready, t + 1)
                        pe.wait_ge(v_diag_ready, t + 1)
                        for j in range(J8):
                            for r in range(R4):
                                c = prob_block(r, j)
                                last = pe.matmul(ps_s[32 * r:32 * r + 32, j * D:(j + 1) * D],
                                                 v_diag[:, (j * R4 + r) * 32:(j * R4 + r + 1) * 32],
                                                 probs_t[:, c:c + D], start=True, stop=True)
                        last.then_inc(heads_done, 1)
                    if ok(i) and not is_int(i, 0):
                        projection_transposes(i, ok)
                    if is_int(i, NT):
                        early_transposes(0)
                main(pe, step)

                def finish_step(i, par, ok, todo):
                    if todo(i + 1):
                        n = (par + 1) % 2
                        pe.wait_ge(f_y, i + 2)
                        wait(pe, f_lo, i + 1)
                        if is_int(i, EARLY):
                            pe.wait_ge(m_mask, 2)
                        transposes(pe, y_tok[n]).then_inc(f_t, 1)
                    if is_int(i, EARLY - 1):
                        pe.wait_ge(f_lo, EARLY + 1)
                        select_tensor(pe, 1, ps_t_flat)
                    if todo(i):
                        pe.wait_ge(f_lo, i + 1)
                        if is_int(i, EARLY):
                            pe.wait_ge(c_read, NT)
                        else:
                            wait(pe, f_read, 2 * (i - 1))
                        for h in range(2):
                            cols = slice(h * HALF, (h + 1) * HALF)
                            product(pe, f_acc(i, par)[:, cols], y_hi[par], y_lo[par], w_hi, w_lo,
                                    cols).then_inc(f_ffn, 1)
                finish(pe, finish_step)



_INS = ["L0_attn_x", "L0_attn_Wq", "L0_attn_bq", "L0_attn_Wk", "L0_attn_bk", "L0_attn_Wv", "L0_attn_bv",
        "L0_ffn_weight", "L0_ffn_bias", "L0_ffn_centroids", "L0_ffn_assignments"]


def kernel(**inputs):
    import numpy as _np
    import concourse.bacc as _bacc
    from concourse import mybir as _mybir
    from concourse.bass_utils import run_bass_kernel_spmd as _run

    nc = _bacc.Bacc("TRN2", target_bir_lowering=False, num_devices=1)
    arrays, args = {}, []
    for name in _INS:
        a = _np.ascontiguousarray(inputs[name])
        arrays[f"in_{name}"] = a
        args.append(nc.dram_tensor(f"in_{name}", a.shape, _mybir.dt.from_np(a.dtype), kind="ExternalInput").ap())
    shape = arrays["in_L0_attn_x"].shape
    args.append(nc.dram_tensor("out", shape, _mybir.dt.float32, kind="ExternalOutput").ap())
    macaron_kernel(nc, *args)
    r = _run(nc, [arrays], core_ids=[0])
    return r.results[0]["out"]
```
